# Optimizing a Trainium2 kernel written in Bass

```python
import numpy as np
import jax
import jax.numpy as jnp

def _softmax(x, axis=-1):
    return jax.nn.softmax(x, axis=axis)

def _gelu(x):
    return jax.nn.gelu(x, approximate=True)

def _silu(x):
    return jax.nn.silu(x)

def _sigmoid(x):
    return jax.nn.sigmoid(x)

def _layernorm(x, axis=-1, eps=1e-05):
    m = jnp.mean(x, axis=axis, keepdims=True)
    v = jnp.var(x, axis=axis, keepdims=True)
    return (x - m) / jnp.sqrt(v + eps)

def _scatter_add(tgt, idx, src, axis=0):
    return tgt.at[idx].add(src)

def _segment_sum(src, seg, n):
    return jax.ops.segment_sum(src, seg, n)
kernel_name = 'mk_flamingo_gated_d2_seqx_r4_e616b3'

def setup_inputs(seed: int=0):
    np.random.seed(seed)
    _w = jnp.asarray

    def _rec_inputs():
        import jax
        import jax.numpy as jnp
        _rk = jax.random.key(seed)
        x = 7.22e-05 + 1 * jax.random.normal(jax.random.fold_in(_rk, 1), (1, 2048, 256), jnp.float32)
        _lenS = 2048 - jax.random.randint(jax.random.fold_in(_rk, 7), (1,), 0, max(1, 2048 // 4) + 1, jnp.int32)
        _lenS2 = 1601 - jax.random.randint(jax.random.fold_in(_rk, 8), (1,), 0, max(1, 1601 // 4) + 1, jnp.int32)
        _ctx_1024P = jax.random.normal(jax.random.fold_in(_rk, 11), (1, 16, 256), jnp.float32)
        _ctx_1024c = jax.random.dirichlet(jax.random.fold_in(_rk, 511), 0.3 * jnp.ones((16,), jnp.float32), (1, 1601))
        _ctx_1024t = jnp.einsum('bsk,bkd->bsd', _ctx_1024c, _ctx_1024P)
        _ctx_1024t = _ctx_1024t * jax.lax.rsqrt(jnp.mean(jnp.square(_ctx_1024t)) + 1e-12) * 0.953939
        ctx_1024 = 4.13588e-05 + 0.999923 * (_ctx_1024t + 0.3 * jax.random.normal(jax.random.fold_in(_rk, 611), (1, 1601, 256), jnp.float32))
        itok_BxS2_0_2047 = jax.random.randint(jax.random.fold_in(_rk, 12), (1, 1601), 0, 512, jnp.int32)
        _g = jax.random.normal(jax.random.fold_in(_rk, 9001), (2, 2), jnp.float32)
        _g = jnp.sign(_g) * jnp.maximum(jnp.abs(_g), 1.0) + (_g == 0) * 1.0
        g_xattn = _g[0]
        g_ffn = _g[1]
        return (x, ctx_1024, itok_BxS2_0_2047, g_xattn, g_ffn)
    x, ctx_1024, itok_BxS2_0_2047, g_xattn, g_ffn = _rec_inputs()

    def _L0_xattn_setup():
        import jax, jax.numpy as jnp
        import numpy as np
        DIM = 256
        HEADS = 16
        HEAD_DIM = DIM // HEADS
        SCALE = HEAD_DIM ** (-0.5)
        key = jax.random.key(seed)
        ks = jax.random.split(key, 13)
        B, Nq, Nk = (4, 512, 512)
        s = DIM ** (-0.5)
        return {'query': jax.random.normal(ks[0], (B, Nq, DIM), jnp.float32), 'key': jax.random.normal(ks[1], (B, Nk, DIM), jnp.float32), 'value': jax.random.normal(ks[2], (B, Nk, DIM), jnp.float32), 'qpos': jax.random.randint(ks[3], (B, Nq), 0, Nq), 'kpos': jax.random.randint(ks[4], (B, Nk), 0, Nk), 'Wq': jax.random.normal(ks[5], (DIM, DIM), jnp.float32) * s, 'bq': jnp.zeros((DIM,), jnp.float32), 'Wk': jax.random.normal(ks[6], (DIM, DIM), jnp.float32) * s, 'bk': jnp.zeros((DIM,), jnp.float32), 'Wv': jax.random.normal(ks[7], (DIM, DIM), jnp.float32) * s, 'bv': jnp.zeros((DIM,), jnp.float32), 'Wo': jax.random.normal(ks[8], (DIM, DIM), jnp.float32) * s, 'bo': jnp.zeros((DIM,), jnp.float32)}
    _L0_xattn_all = _L0_xattn_setup()
    _L0_xattn_in = {k: v for k, v in _L0_xattn_all.items() if k in ('Wq', 'bq', 'Wk', 'bk', 'Wv', 'bv', 'Wo', 'bo')}
    del _L0_xattn_all

    def _L0_ffn_setup():
        import jax, jax.numpy as jnp
        import numpy as np
        D_MODEL = 256
        D_FF = 704
        N_EXPERTS = 8
        key = jax.random.key(seed)
        k_in, k1, k2, k3 = jax.random.split(key, 4)
        scale = 0.02
        inputs = jax.random.normal(k_in, (4, N_EXPERTS * 512, D_MODEL), dtype=jnp.float32)
        w1 = jax.random.normal(k1, (N_EXPERTS, D_MODEL, D_FF), dtype=jnp.float32) * scale
        w3 = jax.random.normal(k3, (N_EXPERTS, D_MODEL, D_FF), dtype=jnp.float32) * scale
        w2 = jax.random.normal(k2, (N_EXPERTS, D_FF, D_MODEL), dtype=jnp.float32) * scale
        return {'inputs': inputs, 'w1': w1, 'w3': w3, 'w2': w2}
    _L0_ffn_all = _L0_ffn_setup()
    _L0_ffn_in = {k: v for k, v in _L0_ffn_all.items() if k in ('w1', 'w3', 'w2')}
    del _L0_ffn_all

    def _L1_xattn_setup():
        import jax, jax.numpy as jnp
        import numpy as np
        H = 256
        B = 8
        L_CHAR = 512
        L_SUB = 256

        def _linear(x, W, b):
            return jnp.einsum('blh,oh->blo', x, W) + b

        def _interp_linear(x, out_len):
            L_in = x.shape[1]
            pos = (jnp.arange(out_len, dtype=x.dtype) + 0.5) * (L_in / out_len) - 0.5
            pos = jnp.clip(pos, 0.0, L_in - 1)
            lo = jnp.floor(pos).astype(jnp.int32)
            hi = jnp.minimum(lo + 1, L_in - 1)
            w = (pos - lo.astype(x.dtype))[None, :, None]
            return x[:, lo] * (1 - w) + x[:, hi] * w
        key = jax.random.key(seed)
        ks = jax.random.split(key, 18)
        s = 0.02
        inp = {'char_emb': jax.random.normal(ks[0], (B, L_CHAR, H), jnp.float32), 'subword_emb': jax.random.normal(ks[1], (B, L_SUB, H), jnp.float32)}
        names = ['Wq_c', 'Wk_s', 'Wv_s', 'Wq_s', 'Wk_c', 'Wv_c']
        for i, n in enumerate(names):
            inp[n] = jax.random.normal(ks[2 + 2 * i], (H, H), jnp.float32) * s
            inp['b' + n[1:]] = jax.random.normal(ks[3 + 2 * i], (H,), jnp.float32) * s
        inp['Wg'] = jax.random.normal(ks[14], (H, 2 * H), jnp.float32) * s
        inp['bg'] = jax.random.normal(ks[15], (H,), jnp.float32) * s
        return inp
    _L1_xattn_all = _L1_xattn_setup()
    _L1_xattn_in = {k: v for k, v in _L1_xattn_all.items() if k in ('Wq_c', 'bq_c', 'Wk_s', 'bk_s', 'Wv_s', 'bv_s', 'Wq_s', 'bq_s', 'Wk_c', 'bk_c', 'Wv_c', 'bv_c', 'Wg', 'bg')}
    del _L1_xattn_all

    def _L1_ffn_setup():
        import jax, jax.numpy as jnp
        import numpy as np
        B, N, D = (4, 512, 256)
        SPARSITY = 0.01
        key = jax.random.key(seed)
        k1, k2, k3 = jax.random.split(key, 3)
        x = jax.random.normal(k1, (B, N, D), dtype=jnp.float32)
        spatial = jax.random.normal(k2, (D, D), dtype=jnp.float32) * 0.02
        freq = jnp.fft.fft(spatial, axis=-1)
        k = int(D * SPARSITY)
        mag = jnp.abs(freq)
        kth = jax.lax.top_k(mag, k)[0][:, -1:]
        w_sparse = jnp.where(mag >= kth, freq, 0.0 + 0j)
        bias = jax.random.normal(k3, (D,), dtype=jnp.float32) * 0.01
        return {'x': x, 'w_freq_real': jnp.real(w_sparse).astype(jnp.float32), 'w_freq_imag': jnp.imag(w_sparse).astype(jnp.float32), 'bias': bias}
    _L1_ffn_all = _L1_ffn_setup()
    _L1_ffn_in = {k: v for k, v in _L1_ffn_all.items() if k in ('w_freq_real', 'w_freq_imag', 'bias')}
    del _L1_ffn_all
    return {'x': x, 'ctx_1024': ctx_1024, 'itok_BxS2_0_2047': itok_BxS2_0_2047, 'g_xattn': g_xattn, 'g_ffn': g_ffn, 'L0_xattn_Wq': _L0_xattn_in['Wq'], 'L0_xattn_bq': _L0_xattn_in['bq'], 'L0_xattn_Wk': _L0_xattn_in['Wk'], 'L0_xattn_bk': _L0_xattn_in['bk'], 'L0_xattn_Wv': _L0_xattn_in['Wv'], 'L0_xattn_bv': _L0_xattn_in['bv'], 'L0_xattn_Wo': _L0_xattn_in['Wo'], 'L0_xattn_bo': _L0_xattn_in['bo'], 'L0_ffn_w1': _L0_ffn_in['w1'], 'L0_ffn_w3': _L0_ffn_in['w3'], 'L0_ffn_w2': _L0_ffn_in['w2'], 'L1_xattn_Wq_c': _L1_xattn_in['Wq_c'], 'L1_xattn_bq_c': _L1_xattn_in['bq_c'], 'L1_xattn_Wk_s': _L1_xattn_in['Wk_s'], 'L1_xattn_bk_s': _L1_xattn_in['bk_s'], 'L1_xattn_Wv_s': _L1_xattn_in['Wv_s'], 'L1_xattn_bv_s': _L1_xattn_in['bv_s'], 'L1_xattn_Wq_s': _L1_xattn_in['Wq_s'], 'L1_xattn_bq_s': _L1_xattn_in['bq_s'], 'L1_xattn_Wk_c': _L1_xattn_in['Wk_c'], 'L1_xattn_bk_c': _L1_xattn_in['bk_c'], 'L1_xattn_Wv_c': _L1_xattn_in['Wv_c'], 'L1_xattn_bv_c': _L1_xattn_in['bv_c'], 'L1_xattn_Wg': _L1_xattn_in['Wg'], 'L1_xattn_bg': _L1_xattn_in['bg'], 'L1_ffn_w_freq_real': _L1_ffn_in['w_freq_real'], 'L1_ffn_w_freq_imag': _L1_ffn_in['w_freq_imag'], 'L1_ffn_bias': _L1_ffn_in['bias']}

def reference(x, ctx_1024, itok_BxS2_0_2047, g_xattn, g_ffn, L0_xattn_Wq, L0_xattn_bq, L0_xattn_Wk, L0_xattn_bk, L0_xattn_Wv, L0_xattn_bv, L0_xattn_Wo, L0_xattn_bo, L0_ffn_w1, L0_ffn_w3, L0_ffn_w2, L1_xattn_Wq_c, L1_xattn_bq_c, L1_xattn_Wk_s, L1_xattn_bk_s, L1_xattn_Wv_s, L1_xattn_bv_s, L1_xattn_Wq_s, L1_xattn_bq_s, L1_xattn_Wk_c, L1_xattn_bk_c, L1_xattn_Wv_c, L1_xattn_bv_c, L1_xattn_Wg, L1_xattn_bg, L1_ffn_w_freq_real, L1_ffn_w_freq_imag, L1_ffn_bias):
    import jax
    import jax.numpy as jnp

    def _L0_xattn_ref(query, key, value, qpos, kpos, Wq, bq, Wk, bk, Wv, bv, Wo, bo):
        import jax, jax.numpy as jnp
        import numpy as np
        DIM = 256
        HEADS = 16
        HEAD_DIM = DIM // HEADS
        SCALE = HEAD_DIM ** (-0.5)
        B, Nq, C = query.shape

        def split_heads(x):
            return x.reshape(x.shape[0], x.shape[1], HEADS, HEAD_DIM).transpose(0, 2, 1, 3)
        q = split_heads(query @ Wq + bq)
        k = split_heads(key @ Wk + bk)
        v = split_heads(value @ Wv + bv)
        attn = jnp.einsum('bhqd,bhkd->bhqk', q, k) * SCALE
        attn = jax.nn.softmax(attn, axis=-1)
        x = jnp.einsum('bhqk,bhkd->bhqd', attn, v)
        x = x.transpose(0, 2, 1, 3).reshape(B, Nq, C)
        return x @ Wo + bo

    def _L0_ffn_ref(inputs, w1, w3, w2):
        import jax, jax.numpy as jnp
        import numpy as np
        D_MODEL = 256
        D_FF = 704
        N_EXPERTS = 8
        B, T, D = inputs.shape
        E = w1.shape[0]
        C = T // E
        x = inputs.reshape(B, E, C, D)
        gate = jnp.einsum('becd,edf->becf', x, w1)
        up = jnp.einsum('becd,edf->becf', x, w3)
        h = jax.nn.silu(gate) * up
        out = jnp.einsum('becf,efd->becd', h, w2)
        return out.reshape(B, T, D)

    def _L1_xattn_ref(char_emb, subword_emb, Wq_c, bq_c, Wk_s, bk_s, Wv_s, bv_s, Wq_s, bq_s, Wk_c, bk_c, Wv_c, bv_c, Wg, bg):
        import jax, jax.numpy as jnp
        import numpy as np
        H = 256
        B = 8
        L_CHAR = 512
        L_SUB = 256

        def _linear(x, W, b):
            return jnp.einsum('blh,oh->blo', x, W) + b

        def _interp_linear(x, out_len):
            L_in = x.shape[1]
            pos = (jnp.arange(out_len, dtype=x.dtype) + 0.5) * (L_in / out_len) - 0.5
            pos = jnp.clip(pos, 0.0, L_in - 1)
            lo = jnp.floor(pos).astype(jnp.int32)
            hi = jnp.minimum(lo + 1, L_in - 1)
            w = (pos - lo.astype(x.dtype))[None, :, None]
            return x[:, lo] * (1 - w) + x[:, hi] * w
        h = char_emb.shape[-1]
        scale = 1.0 / jnp.sqrt(jnp.asarray(h, char_emb.dtype))
        Q_char = _linear(char_emb, Wq_c, bq_c)
        K_sub = _linear(subword_emb, Wk_s, bk_s)
        V_sub = _linear(subword_emb, Wv_s, bv_s)
        scores = jnp.einsum('bqh,bkh->bqk', Q_char, K_sub) * scale
        char2sub = jnp.einsum('bqk,bkh->bqh', jax.nn.softmax(scores, axis=-1), V_sub)
        Q_sub = _linear(subword_emb, Wq_s, bq_s)
        K_char = _linear(char_emb, Wk_c, bk_c)
        V_char = _linear(char_emb, Wv_c, bv_c)
        scores2 = jnp.einsum('bqh,bkh->bqk', Q_sub, K_char) * scale
        sub2char = jnp.einsum('bqk,bkh->bqh', jax.nn.softmax(scores2, axis=-1), V_char)
        L_char = char_emb.shape[1]
        if sub2char.shape[1] != L_char:
            sub2char = _interp_linear(sub2char, L_char)
        gate_in = jnp.concatenate([char2sub, sub2char], axis=-1)
        gate = jax.nn.sigmoid(jnp.einsum('blh,oh->blo', gate_in, Wg) + bg)
        return gate * char2sub + (1 - gate) * sub2char

    def _L1_ffn_ref(x, w_freq_real, w_freq_imag, bias):
        import jax, jax.numpy as jnp
        import numpy as np
        B, N, D = (4, 512, 256)
        SPARSITY = 0.01
        w = jax.lax.complex(w_freq_real, w_freq_imag)
        x_freq = jnp.fft.fft(x, axis=-1)
        y_freq = jnp.einsum('bnd,do->bno', x_freq, w)
        y = jnp.real(jnp.fft.ifft(y_freq, axis=-1))
        return y + bias
    x = x + jnp.tanh(g_xattn[0]) * _L0_xattn_ref(_layernorm(x, axis=-1), ctx_1024, ctx_1024, itok_BxS2_0_2047, itok_BxS2_0_2047, L0_xattn_Wq, L0_xattn_bq, L0_xattn_Wk, L0_xattn_bk, L0_xattn_Wv, L0_xattn_bv, L0_xattn_Wo, L0_xattn_bo)
    x = x + jnp.tanh(g_ffn[0]) * _L0_ffn_ref(_layernorm(x, axis=-1), L0_ffn_w1, L0_ffn_w3, L0_ffn_w2)
    x = x + jnp.tanh(g_xattn[1]) * _L1_xattn_ref(_layernorm(x, axis=-1), ctx_1024, L1_xattn_Wq_c, L1_xattn_bq_c, L1_xattn_Wk_s, L1_xattn_bk_s, L1_xattn_Wv_s, L1_xattn_bv_s, L1_xattn_Wq_s, L1_xattn_bq_s, L1_xattn_Wk_c, L1_xattn_bk_c, L1_xattn_Wv_c, L1_xattn_bv_c, L1_xattn_Wg, L1_xattn_bg)
    x = x + jnp.tanh(g_ffn[1]) * _L1_ffn_ref(_layernorm(x, axis=-1), L1_ffn_w_freq_real, L1_ffn_w_freq_imag, L1_ffn_bias)
    return x

_drawn_inputs = setup_inputs


def setup_inputs(seed=0):
    import zlib

    import numpy as np

    out = dict(_drawn_inputs(seed))
    spreads = {'g_ffn': (-1.0, 0.2),
     'L0_xattn_bq': (0.0, 0.52),
     'L0_xattn_bk': (0.0, 2.0),
     'L0_xattn_bv': (0.0, 0.1),
     'L0_xattn_bo': (0.0, 0.1)}
    factors = {'L0_ffn_w1': 2.95,
     'L0_ffn_w3': 2.916,
     'L0_ffn_w2': 2.915,
     'L1_xattn_Wq_c': 8.0,
     'L1_xattn_bq_c': 26.302,
     'L1_xattn_Wk_s': 8.0,
     'L1_xattn_bk_s': 64.0,
     'L1_xattn_bv_s': 6.512,
     'L1_xattn_Wq_s': 8.0,
     'L1_xattn_bq_s': 34.488,
     'L1_xattn_Wk_c': 8.0,
     'L1_xattn_bk_c': 64.0,
     'L1_xattn_bv_c': 6.195,
     'L1_xattn_Wg': 8.0,
     'L1_xattn_bg': 46.222,
     'L1_ffn_bias': 8.0}
    for name, (base, spread) in spreads.items():
        noise = np.random.default_rng([zlib.crc32(name.encode()), seed]).standard_normal(out[name].shape)
        drawn = base * np.exp(spread * noise) if base else spread * noise
        out[name] = jnp.asarray(drawn.astype(out[name].dtype))
    for name, factor in factors.items():
        out[name] = (out[name] * factor).astype(out[name].dtype)
    return out
```

```python
from contextlib import ExitStack

import concourse.bass as bass
from concourse import mybir

F32 = mybir.dt.float32
BF16 = mybir.dt.bfloat16
ALU = mybir.AluOpType
ACT = mybir.ActivationFunctionType
AX = mybir.AxisListType

P = 128
T = 2048
D = 256
DK = D // P
S = 1601
NT = T // P
NS = -(-S // P)
SP_ = NS * P
STAIL = S - (NS - 1) * P
H = 16
HD = D // H
E = 8
EW = T // E
F = 704
NF = -(-F // P)
FTAIL = F - (NF - 1) * P
EPS = 1e-5
SC0 = HD ** -0.5
SC1 = D ** -0.5

G = 4
QW = T // 2
NB = 2 * (H // G)
TERMS = [(0, 3, 0), (1, 2, 3 * HD), (2, 1, 5 * HD)]
NROW = 6 * HD
MROW = 3
CW = 401
CSTEP = 400
NCH = G * (QW // P) * 2

WQ, WK, WV, WO = range(4)
QC, KS, VS, QS, KC, VC = range(6)
CBQ, CBK, CBKS, CBQS, CBKC, CBQC = range(6)
RBV, RBO, RBVS, RBVC, RBG, RBF = range(6)


class Tensors:
    pass


def flat(ap):
    return ap.rearrange("p a b -> p (a b)")


def build(nc, A):
    with ExitStack() as ctx:
        def sb(name, shape, dt=F32):
            return ctx.enter_context(nc.sbuf_tensor(name, shape, dt))

        def dram(name, shape, dt=F32):
            return nc.dram_tensor(name, shape, dt, kind="Internal").ap()

        m = Tensors()
        m.x_in, m.ctx_T, m.out = A["x_in"], A["ctx_T"], A["out"]
        m.w_l0, m.w_l1, m.w_exp, m.wf_T = A["w_l0"], A["w_l1"], A["w_exp"], A["wf_T"]
        m.b_cols, m.b_rows, m.g_in = A["b_cols"], A["b_rows"], A["g_in"]
        m.eye, m.dft, m.interp = A["eye"], A["dft"], A["interp"]
        m.q_parts = dram("q_parts", (3, 2 * D, QW), BF16)
        m.k_parts = dram("k_parts", (3, D, SP_), BF16)
        m.v_blocks = dram("v_blocks", (H // G * P, NS * P))
        m.o_all = dram("o_all", (2, 2 * D, QW))
        m.ks_keep = dram("ks_keep", (P, DK, S))
        m.vs_keep = dram("vs_keep", (P, NS, D))
        m.qs_keep = dram("qs_keep", (NS * P, DK * P))
        m.c2s = dram("c2s", (T, D))
        m.s2c = dram("s2c", (SP_, D))

        m.x = sb("x_rows", [P, NT, D])
        m.w0 = sb("w_layer0", [P, 4 * DK, D])
        m.w1 = sb("w_layer1", [P, 6 * DK + 4, D])
        m.filt = sb("filter_matrix", [P, DK, D])
        m.rows = sb("bias_rows", [P, 6, D])
        m.cols = sb("bias_cols", [P, 6, DK])
        m.bq_scaled = sb("bq_scaled", [P, DK])
        m.gains = sb("gains", [P, 4])
        m.ident = sb("ident", [P, P])
        m.ident_b = sb("ident_b", [P, P], BF16)
        m.xnT = sb("xn_T", [P, DK, T])
        m.neghalf = sb("neghalf", [P, NT])
        m.eps = sb("eps", [P, 1])

        m.reg_f = sb("region_f", [P, 2 * (2 * DK * F + NF * D)])
        m.reg_a = sb("region_a", [P, 23296])
        at = [0]

        def attn(n, shape, dt=F32):
            size = n // 2 if dt == BF16 else n
            v = m.reg_a[:, at[0]:at[0] + size]
            at[0] += size
            return v.bitcast(dt) if dt == BF16 else v

        m.kst, m.qst, m.vb = [], [], []
        for _ in range(2):
            m.kst.append(attn(G * SP_, None, BF16).rearrange("p (h n) -> p h n", h=G))
            m.qst.append(attn(G * QW, None, BF16).rearrange("p (h n) -> p h n", h=G))
            m.vb.append(attn(NS * P, None).rearrange("p (k n) -> p k n", k=NS))
        m.prob = [attn(G * QW, None).rearrange("p (h n) -> p h n", h=G) for _ in range(2)]
        m.oT = attn(QW, None).rearrange("p (b n) -> p b n", b=2)
        m.mx = sb("chunk_maxima", [P, NCH])
        m.mx1 = sb("maxima", [P, NCH // 2])
        m.mrest = sb("maxima_rest", [P, NCH // 2])
        m.mparts = sb("maxima_parts", [P, MROW, NCH // 2], BF16)
        m.mT = sb("maxima_rows", [P, P], BF16)

        phase1(nc, m)
        phase2(nc, m)
        phase3(nc, m)
        phase4(nc, m)
        phase5(nc, m)
        attention1(nc, m, "tok", NT, S, NS)
        attention1(nc, m, "ctx", NS, T, NT)
        phase8(nc, m)


def wait_apart(eng, sem, value, passed):
    eng.wait_ge(sem, value)
    eng.sem_inc(passed, 1)


def region(base, at, shape):
    n = 1
    for s in shape[1:]:
        n *= s
    v = base[:, at:at + n]
    if len(shape) == 3:
        v = v.rearrange("p (a b) -> p a b", b=shape[2])
    elif len(shape) == 4:
        v = v.rearrange("p (a b c) -> p a b c", b=shape[2], c=shape[3])
    return v, at + n


def phase1(nc, m):
    with ExitStack() as ctx:
        def sem(name):
            return ctx.enter_context(nc.semaphore("p1_" + name))

        def ps(name, shape, dt=F32):
            return ctx.enter_context(nc.psum_tensor("p1_" + name, shape, dt))

        proj = ps("proj", [P, 3, 512])
        vps = ps("vps", [P, 2, 512])
        tps = ps("tps", [P, 2, 512])
        ctxT, _ = region(m.reg_f, 0, [P, DK, SP_])
        base = m.reg_a
        a0 = (G * SP_ + G * QW) // 2 + NS * P
        xf, a0 = region(base, a0, [P, 2, 512])
        r1, a0 = region(base, a0, [P, 2, 512])
        parts = base[:, a0:a0 + 2 * 3 * 256].bitcast(BF16).rearrange("p (s a n) -> p s a n", s=2, a=3)
        a0 = 2 * ((G * SP_ + G * QW) // 2 + NS * P)
        vaug, a0 = region(base, a0, [P, NS, H, 32])
        xn, a0 = region(base, 2 * ((G * SP_ + G * QW) // 2 + NS * P) + 2 * G * QW, [P, 2, D])
        stats = ctx.enter_context(nc.sbuf_tensor("p1_stats", [P, NT, 6], F32))
        mv = ctx.enter_context(nc.sbuf_tensor("p1_mv", [P, NT, 2], F32))
        var = ctx.enter_context(nc.sbuf_tensor("p1_var", [P, NT], F32))
        rstd = ctx.enter_context(nc.sbuf_tensor("p1_rstd", [P, NT], F32))
        gin = ctx.enter_context(nc.sbuf_tensor("p1_gin", [P, 4], F32))

        s_ctx, s_w0, s_cols, s_x, s_rows, s_ident, s_late, s_gin = (
            sem(n) for n in ("ctx", "w0", "cols", "x", "rows", "ident", "late", "gin"))
        s_bq, s_stats, s_aggr, s_var, s_rstd, s_norm = (
            sem(n) for n in ("bq", "stats", "aggr", "var", "rstd", "norm"))
        s_xT, s_xTcopy, s_proj, s_p1, s_r1, s_p2, s_p3 = (
            sem(n) for n in ("xT", "xTcopy", "proj", "p1", "r1", "p2", "p3"))
        s_vproj, s_vbias, s_const, s_vout, s_gain = (sem(n) for n in ("vproj", "vbias", "const", "vout", "gain"))
        s_pout = [sem(f"pout{i}") for i in range(2)]

        def chunk(g):
            if g < 8:
                return WK, g // 4, (g % 4) * 512, min(512, S - (g % 4) * 512)
            return WQ, g % 2, ((g - 8) // 2) * 512, 512

        def stored(g):
            return 16 * sum(1 if c < 8 else 2 for c in range(g % 2, g, 2))

        block = ctx.enter_context(nc.Block())

        @block.sync
        def _(sp):
            sp.dma_start(ctxT, m.ctx_T).then_inc(s_ctx, 16)
            sp.dma_start(m.w0[:, :, :], m.w_l0).then_inc(s_w0, 16)
            sp.dma_start(m.cols[:, :, :], m.b_cols).then_inc(s_cols, 16)
            sp.dma_start(m.x[:, :, :], m.x_in.rearrange("(t p) d -> p t d", p=P)).then_inc(s_x, 16)
            sp.dma_start(m.rows[:, :, :], m.b_rows.to_broadcast([P, 6, D])).then_inc(s_rows, 16)
            sp.dma_start(m.ident[:, :], m.eye).then_inc(s_ident, 16)
            sp.dma_start(gin[:, :], m.g_in.to_broadcast([P, 4])).then_inc(s_gin, 16)
            sp.dma_start(m.w1[:, :, :], m.w_l1).then_inc(s_late, 16)
            for g in range(16):
                _, mt, col, w = chunk(g)
                sp.wait_ge(s_p3, g + 1)
                src = parts[:, g % 2, :, 0:w]
                if g < 8:
                    w = min(512, SP_ - col)
                    dst = m.k_parts.rearrange("a r n -> r a n")[mt * P:mt * P + P, :, col:col + w]
                    sp.dma_start(dst, parts[:, g % 2, :, 0:w]).then_inc(s_pout[g % 2], 16)
                else:
                    for c in range(2):
                        r = c * D + mt * P
                        dst = m.q_parts.rearrange("a r n -> r a n")[r:r + P, :, col // 2:col // 2 + EW]
                        sp.dma_start(dst, src[:, :, c * EW:(c + 1) * EW]).then_inc(s_pout[g % 2], 16)
            sp.wait_ge(s_pout[0], stored(16))
            sp.wait_ge(s_pout[1], stored(17))
            sp.wait_ge(s_late, 16)

        @block.gpsimd
        def _(pool):
            pool.memset(vaug[:, :, :, 0:HD], 0.0).then_inc(s_const, 1)
            pool.memset(vaug[:, 0:NS - 1, :, HD:], 1.0).then_inc(s_const, 1)
            pool.memset(vaug[:, NS - 1, :, HD:], 0.0).then_inc(s_const, 1)
            pool.wait_ge(s_const, 3)
            pool.memset(vaug[0:STAIL, NS - 1, :, HD:], 1.0).then_inc(s_const, 1)
            pool.memset(m.neghalf[:, :], -0.5).then_inc(s_const, 1)
            pool.wait_ge(s_const, 5)
            pool.wait_ge(s_var, 1)
            pool.tensor_tensor(rstd[:, :], var[:, :], m.neghalf[:, :], ALU.pow).then_inc(s_rstd, 1)
            pool.wait_ge(s_rstd, 1)
            ones_rows(pool, m, 0, s_const, 5)
            pool.wait_ge(s_vbias, NS)
            for i in range(H // G):
                dst = m.v_blocks[i * P:(i + 1) * P, :].rearrange("p (k h n) -> p k h n", k=NS, h=G)
                pool.dma_start(dst, vaug[:, :, i * G:(i + 1) * G, :]).then_inc(s_vout, 16)
            pool.wait_ge(s_vout, 16 * (H // G))
            pool.wait_ge(s_const, 7)

        @block.vector
        def _(dve):
            dve.wait_ge(s_cols, 16)
            dve.tensor_scalar(m.bq_scaled[:, :], m.cols[:, CBQ, :], SC0, None, ALU.mult).then_inc(s_bq, 1)
            dve.wait_ge(s_x, 16)
            for t in range(NT):
                dve.bn_stats(stats[:, t, :], m.x[:, t, :]).then_inc(s_stats, 1)
            for t in range(NT):
                dve.wait_ge(s_stats, t + 1)
                dve.bn_aggr(mv[:, t, :], stats[:, t, :]).then_inc(s_aggr, 1)
            dve.wait_ge(s_aggr, NT)
            dve.tensor_scalar(var[:, :], mv[:, :, 1], EPS, None, ALU.add).then_inc(s_var, 1)
            dve.wait_ge(s_ident, 16)
            dve.tensor_copy(m.ident_b[:, :], m.ident[:, :])

            def norm(t):
                if t == 0:
                    dve.wait_ge(s_rstd, 1)
                if t >= 2:
                    dve.wait_ge(s_xT, t - 1)
                dve.tensor_scalar(xn[:, t % 2, :], m.x[:, t, :], mv[:, t, 0:1], rstd[:, t:t + 1],
                                  ALU.subtract, ALU.mult).then_inc(s_norm, 1)

            def split(g):
                w = chunk(g)[3]
                p = parts[:, g % 2, :, 0:w]
                dve.wait_ge(s_p1, g + 1)
                if g < 8 and w == STAIL:
                    dve.memset(parts[:, g % 2, :, w:P], 0.0)
                dve.tensor_tensor(r1[:, g % 2, 0:w], xf[:, g % 2, 0:w], p[:, 0, :], ALU.subtract).then_inc(s_r1, 1)
                dve.wait_ge(s_r1, g + 1)
                dve.tensor_copy(p[:, 1, :], r1[:, g % 2, 0:w]).then_inc(s_p2, 1)
                dve.wait_ge(s_p2, g + 1)
                dve.tensor_tensor(p[:, 2, :], r1[:, g % 2, 0:w], p[:, 1, :], ALU.subtract).then_inc(s_p3, 1)

            for n in range(8):
                norm(2 * n)
                norm(2 * n + 1)
                split(n)
            dve.wait_ge(s_rows, 16)
            dve.wait_ge(s_const, 4)
            for kt in range(NS):
                r = P if kt < NS - 1 else STAIL
                dve.wait_ge(s_vproj, kt + 1)
                dve.tensor_tensor(vaug[0:r, kt, :, 0:HD],
                                  vps[0:r, kt % 2, 0:D].rearrange("p (h d) -> p h d", h=H),
                                  m.rows[0:r, RBV, :].rearrange("p (h d) -> p h d", h=H),
                                  ALU.add).then_inc(s_vbias, 1)
            for g in range(8, 16):
                split(g)

        @block.scalar
        def _(act):
            act.wait_ge(s_gin, 16)
            act.activation(m.gains[:, :], gin[:, :], ACT.Tanh).then_inc(s_gain, 1)
            act.wait_ge(s_cols, 16)

            def values(g):
                which, mt, _, w = chunk(g)
                scale = SC0 if which == WQ else 1.0
                bias = m.bq_scaled[:, mt:mt + 1] if which == WQ else m.cols[:, CBK, mt:mt + 1]
                act.wait_ge(s_proj, g + 1)
                if g >= 2:
                    act.wait_ge(s_p3, g - 1)
                    act.wait_ge(s_pout[g % 2], stored(g))
                act.activation(xf[:, g % 2, 0:w], proj[:, g % 3, 0:w], ACT.Identity, bias=bias, scale=scale)
                act.activation(parts[:, g % 2, 0, 0:w], proj[:, g % 3, 0:w], ACT.Identity,
                               bias=bias, scale=scale).then_inc(s_p1, 1)

            def keep_xT(t):
                act.wait_ge(s_xT, t + 1)
                act.copy(m.xnT[:, :, t * P:(t + 1) * P],
                         tps[:, t % 2, 0:D].rearrange("p (k n) -> p k n", k=DK)).then_inc(s_xTcopy, 1)

            for n in range(8):
                values(n)
                keep_xT(2 * n)
                keep_xT(2 * n + 1)
            act.wait_ge(s_bq, 1)
            for g in range(8, 16):
                values(g)

        @block.tensor
        def _(pe):
            def project(g):
                which, mt, col, w = chunk(g)
                rhs = ctxT if which == WK else m.xnT
                if which == WQ:
                    pe.wait_ge(s_xTcopy, col // P + 4)
                if g >= 3:
                    pe.wait_ge(s_p1, g - 2)
                for k in range(DK):
                    mm = pe.matmul(proj[:, g % 3, 0:w], m.w0[:, which * DK + k, mt * P:(mt + 1) * P],
                                   rhs[:, k, col:col + w], start=(k == 0), stop=(k == DK - 1))
                mm.then_inc(s_proj, 1)

            def turn(t):
                pe.wait_ge(s_norm, t + 1)
                if t >= 2:
                    pe.wait_ge(s_xTcopy, t - 1)
                for k in range(DK):
                    mm = pe.transpose(tps[:, t % 2, k * P:(k + 1) * P], xn[:, t % 2, k * P:(k + 1) * P], m.ident[:, :])
                mm.then_inc(s_xT, 1)

            pe.wait_ge(s_ctx, 16)
            pe.wait_ge(s_w0, 16)
            for n in range(8):
                project(n)
                if n == 0:
                    pe.wait_ge(s_ident, 16)
                turn(2 * n)
                turn(2 * n + 1)
            for kt in range(NS):
                if kt >= 2:
                    pe.wait_ge(s_vbias, kt - 1)
                for k in range(DK):
                    mm = pe.matmul(vps[:, kt % 2, 0:D], ctxT[:, k, kt * P:(kt + 1) * P], m.w0[:, WV * DK + k, :],
                                   start=(k == 0), stop=(k == DK - 1))
                mm.then_inc(s_vproj, 1)
            for g in range(8, 16):
                project(g)


def ones_rows(pool, m, par, signal, base):
    pool.memset(m.kst[par][NROW:NROW + MROW, :, S:], 0.0).then_inc(signal, 1)
    pool.wait_ge(signal, base + 1)
    pool.memset(m.kst[par][NROW:NROW + MROW, :, 0:S], 1.0).then_inc(signal, 1)


def load_k(eng, m, i, par, signal):
    rows = m.k_parts[:, bass.ds(i * (G * HD), G * HD), :].rearrange("a (d h) n -> a d (h n)", h=G)
    for _, n, r in TERMS:
        eng.dma_start(flat(m.kst[par][r:r + n * HD, :, :]), rows[0:n]).then_inc(signal, 16)


def load_q(eng, m, i, par, signal):
    for a, n, r in TERMS:
        src = m.q_parts[a:a + 1, bass.ds(par * D + i * (G * HD), G * HD), :].rearrange("a (d h) n -> a d (h n)", h=G)
        eng.dma_start(flat(m.qst[par][r:r + n * HD, :, :]),
                      src.to_broadcast([n, HD, G * QW])).then_inc(signal, 16)


def load_v(eng, m, i, par, signal):
    eng.dma_start(m.vb[par], m.v_blocks[bass.ds(i * P, P), :].rearrange("p (k n) -> p k n", k=NS)).then_inc(signal, 16)


KQ_LOADS = 16 * 2 * len(TERMS)


def chunk_scores(pe, m, par, n, out, signal):
    h, qt, c = n // (2 * (QW // P)), n // 2 % (QW // P), n % 2
    for j in range(2):
        off = (2 * c + j) * CSTEP
        mm = pe.matmul(out[:, j, 0:CW], m.qst[par][0:NROW, h, qt * P:(qt + 1) * P],
                       m.kst[par][0:NROW, h, off:off + CW], start=True, stop=True)
    mm.then_inc(signal, 1)


def minus_maxima(dve, m, s_m, base):
    dve.tensor_reduce(m.mx1[:, :], m.mx[:, :].rearrange("p (u c) -> p u c", c=2), AX.X, ALU.max).then_inc(s_m, 1)
    dve.wait_ge(s_m, base + 1)
    dve.tensor_scalar(m.mparts[:, 0, :], m.mx1[:, :], -1.0, None, ALU.mult).then_inc(s_m, 1)
    dve.wait_ge(s_m, base + 2)
    dve.scalar_tensor_tensor(out=m.mrest[:, :], in0=m.mx1[:, :], scalar=-1.0, in1=m.mparts[:, 0, :],
                             op0=ALU.mult, op1=ALU.subtract).then_inc(s_m, 1)
    dve.wait_ge(s_m, base + 3)
    dve.tensor_copy(m.mparts[:, 1, :], m.mrest[:, :]).then_inc(s_m, 1)
    dve.wait_ge(s_m, base + 4)
    dve.tensor_tensor(m.mparts[:, 2, :], m.mrest[:, :], m.mparts[:, 1, :], ALU.subtract).then_inc(s_m, 1)


def store_maxima_rows(eng, m, par, signal):
    n = NCH // 2
    for j in range(MROW):
        eng.dma_start(m.qst[par][NROW + j:NROW + j + 1, :, :].rearrange("o h (t n) -> o (h t) n", n=P),
                      m.mT[j * n:(j + 1) * n, :]).then_inc(signal, 16)


def phase2(nc, m):
    with ExitStack() as ctx:
        def sem(name):
            return ctx.enter_context(nc.semaphore("p2_" + name))

        slots = [ctx.enter_context(nc.psum_tensor(f"p2_max{i}", [P, 2, 512], F32)) for i in range(2)]
        other = ctx.enter_context(nc.psum_tensor("p2_other", [P, 3, 512], F32))
        turned = ctx.enter_context(nc.psum_tensor("p2_turned", [P, P], BF16))
        ctxT, at = region(m.reg_f, 0, [P, DK, SP_])
        dft, at = region(m.reg_f, at, [P, 5 * DK, D])
        wT, at = region(m.reg_f, at, [P, 2 * DK, D])
        mid, at = region(m.reg_f, at, [P, 2 * DK, D])
        stage, _ = region(m.reg_a, 2 * ((G * SP_ + G * QW) // 2 + NS * P), [P, 3, 512])

        s_load, s_dft, s_pads, s_mscore, s_mread, s_m, s_turn, s_mcopy, s_mrow = (
            sem(n) for n in ("load", "dft", "pads", "mscore", "mread", "m", "turn", "mcopy", "mrow"))
        s_unit, s_act, s_dve, s_vload = (sem(n) for n in ("unit", "act", "dve", "vload"))
        s_stage = [sem(f"stage{i}") for i in range(3)]

        COS, SIN, COSD, SIND, NSIND = range(5)
        units = [("k", mt, c) for mt in range(DK) for c in range(4)]
        units += [("q", mt, c) for mt in range(DK) for c in range(4)]
        units += [("v", kt, 0) for kt in range(NS)]
        nstore = len(units)
        units += [("a", mt, 0) for mt in range(DK)] + [("b", mt, 0) for mt in range(DK)]
        units += [("f", mt, 0) for mt in range(DK)]
        nu = len(units)
        by_dve = [sum(x[0] == "v" for x in units[:u]) for u in range(nu + 1)]
        by_act = [u - by_dve[u] for u in range(nu + 1)]

        def after(n):
            return range(n * nu // NCH, (n + 1) * nu // NCH)

        def wait_read(eng, u):
            if units[u][0] == "v":
                eng.wait_ge(s_dve, by_dve[u + 1])
            else:
                eng.wait_ge(s_act, by_act[u + 1])

        block = ctx.enter_context(nc.Block())

        @block.sync
        def _(sp):
            load_k(sp, m, 0, 0, s_load)
            load_q(sp, m, 0, 0, s_load)
            load_v(sp, m, 0, 0, s_vload)
            sp.dma_start(dft, m.dft).then_inc(s_dft, 16)
            sp.dma_start(wT, m.wf_T).then_inc(s_dft, 16)
            for u, (kind, a, c) in enumerate(units[:nstore]):
                wait_read(sp, u)
                w = min(512, S - c * 512)
                if kind == "k":
                    dst, src = m.ks_keep[:, a, c * 512:c * 512 + w], stage[:, u % 3, 0:w]
                elif kind == "q":
                    n = 4 if c < 3 else 1
                    dst = m.qs_keep.rearrange("(t p) (k n) -> p t k n", p=P, k=DK)[:, 4 * c:4 * c + n, a, :]
                    src = stage[:, u % 3, 0:n * P].rearrange("p (t n) -> p t n", t=n)
                else:
                    dst, src = m.vs_keep[:, a, :], stage[:, u % 3, 0:D]
                sp.dma_start(dst, src).then_inc(s_stage[u % 3], 16)
            sp.wait_ge(s_mcopy, 1)
            store_maxima_rows(sp, m, 0, s_mrow)
            sp.wait_ge(s_mrow, 16 * MROW)
            sp.wait_ge(s_vload, 16)
            for i in range(3):
                sp.wait_ge(s_stage[i], 16 * len(range(i, nstore, 3)))

        @block.gpsimd
        def _(pool):
            ones_rows(pool, m, 1, s_pads, 0)
            pool.wait_ge(s_pads, 2)

        @block.vector
        def _(dve):
            for n in range(NCH):
                dve.wait_ge(s_mscore, n + 1)
                dve.tensor_reduce(m.mx[:, n:n + 1], slots[n % 2][:, :, 0:CW], AX.XY, ALU.max).then_inc(s_mread, 1)
                for u in after(n):
                    if units[u][0] == "v":
                        dve.wait_ge(s_unit, u + 1)
                        dve.wait_ge(s_stage[u % 3], 16 * (u // 3))
                        dve.tensor_tensor(stage[:, u % 3, 0:D], other[:, u % 3, 0:D], m.rows[:, RBVS, :],
                                          ALU.add).then_inc(s_dve, 1)
            dve.wait_ge(s_mread, NCH)
            minus_maxima(dve, m, s_m, 0)
            dve.wait_ge(s_turn, 1)
            dve.tensor_copy(m.mT[0:MROW * NCH // 2, :], turned[0:MROW * NCH // 2, :]).then_inc(s_mcopy, 1)

        @block.scalar
        def _(act):
            for u, (kind, a, c) in enumerate(units):
                if kind == "v":
                    continue
                act.wait_ge(s_unit, u + 1)
                if u < nstore and u >= 3:
                    act.wait_ge(s_stage[u % 3], 16 * (u // 3))
                if kind in "kq":
                    w = 512 if c < 3 else (STAIL if kind == "k" else P)
                    bias = m.cols[:, CBKS if kind == "k" else CBQS, a:a + 1]
                    ins = act.activation(stage[:, u % 3, 0:w], other[:, u % 3, 0:w], ACT.Identity, bias=bias)
                else:
                    out = m.filt[:, a, :] if kind == "f" else mid[:, (0 if kind == "a" else DK) + a, :]
                    ins = act.copy(out, other[:, u % 3, 0:D])
                ins.then_inc(s_act, 1)

        @block.tensor
        def _(pe):
            def unit(u):
                kind, a, c = units[u]
                if u >= 3:
                    wait_read(pe, u - 3)
                out = other[:, u % 3, :]
                rows = slice(a * P, (a + 1) * P)
                if kind in "kq":
                    w = 512 if c < 3 else (STAIL if kind == "k" else P)
                    wn = KS if kind == "k" else QS
                    pairs = [(m.w1[:, wn * DK + k, rows], ctxT[:, k, c * 512:c * 512 + w]) for k in range(DK)]
                elif kind == "v":
                    w = D
                    pairs = [(ctxT[:, k, rows], m.w1[:, VS * DK + k, :]) for k in range(DK)]
                elif kind in "ab":
                    w = D
                    re, im = (COSD, NSIND) if kind == "a" else (SIND, COSD)
                    pairs = [(wT[:, k, rows], dft[:, re * DK + k, :]) for k in range(DK)]
                    pairs += [(wT[:, DK + k, rows], dft[:, im * DK + k, :]) for k in range(DK)]
                else:
                    w = D
                    pairs = [(dft[:, COS * DK + k, rows], mid[:, k, :]) for k in range(DK)]
                    pairs += [(dft[:, SIN * DK + k, rows], mid[:, DK + k, :]) for k in range(DK)]
                if kind == "a" and a == 0:
                    pe.wait_ge(s_dft, 32)
                if kind == "f" and a == 0:
                    pe.wait_ge(s_act, by_act[u])
                for i, (l, r) in enumerate(pairs):
                    mm = pe.matmul(out[:, 0:w], l, r, start=(i == 0), stop=(i == len(pairs) - 1))
                mm.then_inc(s_unit, 1)

            pe.wait_ge(s_load, KQ_LOADS)
            for n in range(NCH):
                if n >= 2:
                    pe.wait_ge(s_mread, n - 1)
                chunk_scores(pe, m, 0, n, slots[n % 2], s_mscore)
                for u in after(n):
                    unit(u)
            pe.wait_ge(s_m, 5)
            pe.transpose(turned[0:MROW * NCH // 2, :], flat(m.mparts[:, :, :]), m.ident_b[:, :]).then_inc(s_turn, 1)


def phase3(nc, m):
    with ExitStack() as ctx:
        def sem(name):
            return ctx.enter_context(nc.semaphore("p3_" + name))

        sps = ctx.enter_context(nc.psum_tensor("p3_scores", [P, 2, 512], F32))
        ops = ctx.enter_context(nc.psum_tensor("p3_out", [P, 2, 512], F32))
        slots = [ctx.enter_context(nc.psum_tensor(f"p3_max{i}", [P, 2, 512], F32)) for i in range(2)]
        turned = slots[0][:, 0, 0:P // 2].bitcast(BF16)

        s_scores, s_exp, s_pv, s_done, s_oevac = (sem(n) for n in ("scores", "exp", "pv", "done", "oevac"))
        s_mscore, s_mread, s_m, s_turn, s_mcopy, s_mrow, s_ostore = (
            sem(n) for n in ("mscore", "mread", "m", "turn", "mcopy", "mrow", "ostore"))
        s_kqdone, s_ofree, s_passed, s_weights = (sem(n) for n in ("kqdone", "ofree", "passed", "weights"))
        s_load, s_vload = ([sem(f"{n}{i}") for i in range(2)] for n in ("load", "vload"))

        UNITS = 2 * G
        PER = NS * UNITS
        PVS = 2 * NS
        PVC = 4
        J_TURN = 4
        U_MAX = (11, 94)

        def max_chunks(u):
            return [n for n in range(NCH) if U_MAX[0] + n * (U_MAX[1] - U_MAX[0]) // (NCH - 1) == u]

        def blocks(eng, body):
            with eng.Fori(0, NB // 2 - 1) as i:
                body(i * 2, 0, i, True)
                body(i * 2 + 1, 1, i, True)
            body(NB - 2, 0, NB // 2 - 1, True)
            body(NB - 1, 1, NB // 2 - 1, False)

        block = ctx.enter_context(nc.Block())

        @block.sync
        def _(sp):
            sp.sem_inc(s_mrow, 16 * MROW)
            sp.sem_inc(s_vload[0], 16)

            def body(b, par, i, more):
                if more:
                    sp.wait_ge(s_kqdone, b + 1)
                    load_k(sp, m, i + par, 1 - par, s_load[1 - par])
                    load_q(sp, m, i + par, 1 - par, s_load[1 - par])
                    sp.wait_ge(s_done, b + 1)
                    load_v(sp, m, i + par, 1 - par, s_vload[1 - par])
                    if isinstance(b, int):
                        for e in range(2):
                            sp.dma_start(expert_weights(m, e), m.w_exp[e * P:(e + 1) * P, :]).then_inc(s_weights, 16)
                    sp.wait_ge(s_mcopy, b + 2)
                    store_maxima_rows(sp, m, 1 - par, s_mrow)

            blocks(sp, body)
            sp.wait_ge(s_weights, 32)

        @block.gpsimd
        def _(pool):
            def body(b, par, i, more):
                wait_apart(pool, s_oevac, 2 * b + 4, s_passed)
                for h in range(G):
                    dst = m.o_all[:, bass.ds(par * D + i * (G * HD) + h * HD, HD), :]
                    pool.dma_start(dst, flat(m.oT[32 * h:32 * (h + 1), :, :])).then_inc(s_ostore, 16)
                pool.wait_ge(s_ostore, (b + 1) * (16 * G))
                pool.sem_inc(s_ofree, 1)

            blocks(pool, body)

        @block.vector
        def _(dve):
            dve.sem_inc(s_mread, 2)
            dve.sem_inc(s_mcopy, 1)

            def body(b, par, i, more):
                if not more:
                    return
                for n in range(NCH):
                    dve.wait_ge(s_mscore, b * NCH + n + 1)
                    dve.tensor_reduce(m.mx[:, n:n + 1], slots[n % 2][:, :, 0:CW], AX.XY, ALU.max).then_inc(s_mread, 1)
                dve.wait_ge(s_mread, b * NCH + NCH + 2)
                minus_maxima(dve, m, s_m, b * 5)
                dve.wait_ge(s_turn, b + 1)
                dve.wait_ge(s_mrow, (b + 1) * (16 * MROW))
                dve.tensor_copy(m.mT[0:MROW * NCH // 2, :], turned[0:MROW * NCH // 2, :]).then_inc(s_mcopy, 1)

            blocks(dve, body)

        @block.scalar
        def _(act):
            act.sem_inc(s_oevac, 2)
            act.sem_inc(s_ofree, 1)

            def body(b, par, i, more):
                for kt in range(NS):
                    buf = m.prob[(par * NS + kt) % 2]
                    for j in range(UNITS):
                        h, qb = j // 2, j % 2
                        u = kt * UNITS + j
                        if h == 0:
                            act.wait_ge(s_pv, b * PVS + 2 * kt + qb + 1)
                        act.wait_ge(s_scores, b * PER + u + 1)
                        act.activation(buf[:, h, qb * 512:(qb + 1) * 512], sps[:, u % 2, :], ACT.Exp).then_inc(s_exp, 1)
                act.wait_ge(s_ofree, b + 1)
                for qb in range(2):
                    act.wait_ge(s_pv, b * PVS + PVS + PVC - 1 + qb)
                    act.copy(m.oT[:, qb, :], ops[:, qb, :]).then_inc(s_oevac, 1)

            blocks(act, body)

        @block.tensor
        def _(pe):
            pe.sem_inc(s_pv, PVC)
            pe.sem_inc(s_kqdone, 1)
            pe.sem_inc(s_done, 1)

            def pv(b, par, i, kt, quarter):
                qb, first = quarter // 2, quarter % 2 == 0
                if first:
                    pe.wait_ge(s_exp, b * PER + kt * UNITS + 2 * (G - 1) + qb + 1)
                if kt == 0 and quarter == 0:
                    pe.wait_ge(s_vload[par], i * 16 + 16)
                if kt == 0 and first:
                    pe.wait_ge(s_oevac, b * 2 + qb + 1)
                buf = m.prob[(par * NS + kt) % 2]
                half = slice(quarter % 2 * 256, quarter % 2 * 256 + 256)
                for h in range(G):
                    mm = pe.matmul(ops[32 * h:32 * h + 32, qb, half], m.vb[par][:, kt, 32 * h:32 * h + 32],
                                   buf[:, h, quarter * 256:quarter * 256 + 256],
                                   start=(kt == 0 and first), stop=(kt == NS - 1), skip_group_check=True)
                    if kt == NS - 1 and quarter == 0 and h == 0:
                        mm.then_inc(s_kqdone, 1)
                if not first:
                    mm.then_inc(s_pv, 1)

            def body(b, par, i, more):
                pe.wait_ge(s_mrow, (b + 1) * (16 * MROW))
                for kt in range(NS):
                    for j in range(UNITS):
                        h, qb = j // 2, j % 2
                        u = kt * UNITS + j
                        if u >= 2:
                            pe.wait_ge(s_exp, b * PER + u - 1)
                        pe.matmul(sps[:, u % 2, :], m.kst[par][0:NROW + MROW, h, kt * P:(kt + 1) * P],
                                  m.qst[par][0:NROW + MROW, h, qb * 512:(qb + 1) * 512],
                                  start=True, stop=True).then_inc(s_scores, 1)
                        for n in max_chunks(u) if more else []:
                            if n == 0:
                                pe.wait_ge(s_mcopy, b + 1)
                                wait_loaded(pe, i, par)
                            pe.wait_ge(s_mread, b * NCH + n + 1)
                            chunk_scores(pe, m, 1 - par, n, slots[n % 2], s_mscore)
                        if kt >= 1 and j % 2 == 1:
                            pv(b, par, i, kt - 1, j // 2)
                        if more and kt == NS - 1 and j == J_TURN:
                            pe.wait_ge(s_m, b * 5 + 5)
                            pe.transpose(turned[0:MROW * NCH // 2, :], flat(m.mparts[:, :, :]),
                                         m.ident_b[:, :]).then_inc(s_turn, 1)
                for quarter in range(4):
                    pv(b, par, i, NS - 1, quarter)
                pe.drain().then_inc(s_done, 1)

            def wait_loaded(pe, i, par):
                pe.wait_ge(s_load[1 - par], i * KQ_LOADS + KQ_LOADS)

            blocks(pe, body)


def expert_weights(m, par):
    n = 2 * DK * F + NF * D
    return m.reg_f[:, par * n:(par + 1) * n]


def phase4(nc, m):
    with ExitStack() as ctx:
        def sem(name):
            return ctx.enter_context(nc.semaphore("p4_" + name))

        def ps(name):
            return ctx.enter_context(nc.psum_tensor("p4_" + name, [P, 2, 512], F32))

        def small(name, shape):
            return ctx.enter_context(nc.sbuf_tensor("p4_" + name, shape, F32))

        aps, tps, gps, dps = ps("attn"), ps("turn"), ps("gate_up"), ps("down")
        w = [expert_weights(m, i) for i in range(2)]
        w13 = [x[:, 0:2 * DK * F].rearrange("p (a f) -> p a f", f=F) for x in w]
        w2 = [x[:, 2 * DK * F:].rearrange("p (a d) -> p a d", d=D) for x in w]
        at = 0
        oT, at = region(m.reg_a, at, [P, 2, DK, EW])
        den, at = region(m.reg_a, at, [P, 2, DK, EW])
        rec, at = region(m.reg_a, at, [P, DK, EW])
        on, at = region(m.reg_a, at, [P, 2, DK, EW])
        tmp, at = region(m.reg_a, at, [P, 2, D])
        xn2, at = region(m.reg_a, at, [P, 2, D])
        xn3, at = region(m.reg_a, at, [P, 2, D])
        xn2T, at = region(m.reg_a, at, [P, 2, DK, EW])
        sg, at = region(m.reg_a, at, [P, 2, EW])
        hT, at = region(m.reg_a, at, [P, NF, EW])
        st = [small(f"stats{i}", [P, 2, 6]) for i in range(2)]
        mv = [small(f"mv{i}", [P, 2, 2]) for i in range(2)]
        var = [small(f"var{i}", [P, 2]) for i in range(2)]
        rstd = [small(f"rstd{i}", [P, 2]) for i in range(2)]

        s_passed = sem("passed")
        s_w = [sem(f"w{i}") for i in range(2)]
        s_o = [sem(f"o{i}") for i in range(2)]
        s_rec, s_onorm, s_attn, s_bo, s_x1 = (sem(n) for n in ("rec", "onorm", "attn", "bo", "x1"))
        s_turn, s_copy, s_gu, s_silu, s_h, s_down, s_x2 = (
            sem(n) for n in ("turn", "copy", "gu", "silu", "h", "down", "x2"))
        s_st, s_ag, s_var, s_rstd, s_norm = ([sem(f"{n}{i}") for i in range(2)] for n in ("st", "ag", "var", "rstd", "norm"))

        def experts(eng, body):
            body(0, 0, 0, True, False)
            with eng.Fori(0, E // 2 - 1) as i:
                body(i * 2 + 1, 1, i, False, False)
                body(i * 2 + 2, 0, i + 1, False, False)
            body(E - 1, 1, E // 2 - 1, False, True)

        def load_weights(eng, e, par):
            eng.dma_start(w[par], m.w_exp[bass.ds(e * P, P), :]).then_inc(s_w[par], 16)

        def load_attn(eng, par, half):
            for a, dst in enumerate((oT, den)):
                rows = m.o_all[a, par * D:(par + 1) * D, :].rearrange("(k p) n -> p k n", p=P)
                eng.dma_start(dst[:, par, :, :], rows[:, :, bass.ds(half * EW, EW)]).then_inc(s_o[par], 16)

        block = ctx.enter_context(nc.Block())

        @block.sync
        def _(sp):
            load_attn(sp, 0, 0)
            for i in range(2):
                sp.sem_inc(s_w[i], 16)

            def body(e, par, half, first, last):
                if last:
                    return
                if not first:
                    sp.wait_ge(s_onorm, e)
                load_attn(sp, 1 - par, half + par)
                if not first:
                    sp.wait_ge(s_down, e * 2)
                    load_weights(sp, e + 1, 1 - par)

            experts(sp, body)

        @block.gpsimd
        def _(pool):
            def scale(i, n):
                pool.wait_ge(s_var[i], n + 1)
                pool.tensor_tensor(rstd[i][:, :], var[i][:, :], m.neghalf[:, 0:2], ALU.pow).then_inc(s_rstd[i], 1)

            scale(0, 0)

            def body(e, par, half, first, last):
                if not first:
                    scale(1, e - 1)
                if not last:
                    scale(0, e + 1)

            experts(pool, body)
            scale(1, E - 1)

        @block.vector
        def _(dve):
            dve.sem_inc(s_h, 2)
            dve.sem_inc(s_x2, 2)

            def xs(e, t):
                return m.x[:, bass.ds(e * 2 + t, 1), :].rearrange("p o d -> p (o d)")

            def moments(i, e, s_src):
                for t in range(2):
                    wait_apart(dve, s_src, e * 2 + t + (1 if i == 0 else 3), s_passed)
                    dve.bn_stats(st[i][:, t, :], xs(e, t)).then_inc(s_st[i], 1)
                for t in range(2):
                    wait_apart(dve, s_st[i], e * 2 + t + 1, s_passed)
                    dve.bn_aggr(mv[i][:, t, :], st[i][:, t, :]).then_inc(s_ag[i], 1)
                dve.wait_ge(s_ag[i], e * 2 + 2)
                dve.tensor_scalar(var[i][:, :], mv[i][:, :, 1], EPS, None, ALU.add).then_inc(s_var[i], 1)

            def norm(i, e, out):
                dve.wait_ge(s_rstd[i], e + 1)
                for t in range(2):
                    dve.tensor_scalar(out[:, t, :], xs(e, t), mv[i][:, t, 0:1], rstd[i][:, t:t + 1],
                                      ALU.subtract, ALU.mult).then_inc(s_norm[i], 1)

            def attn_result(e, par, half):
                dve.wait_ge(s_o[par], half * 32 + 32)
                dve.reciprocal(rec, den[:, par, :, :]).then_inc(s_rec, 1)
                dve.wait_ge(s_rec, e + 1)
                dve.tensor_tensor(on[:, par, :, :], oT[:, par, :, :], rec, ALU.mult).then_inc(s_onorm, 1)

            def residual1(e):
                for t in range(2):
                    dve.wait_ge(s_attn, e * 2 + t + 1)
                    dve.tensor_tensor(tmp[:, t, :], aps[:, t, 0:D], m.rows[:, RBO, :], ALU.add).then_inc(s_bo, 1)
                for t in range(2):
                    dve.wait_ge(s_bo, e * 2 + t + 1)
                    dve.scalar_tensor_tensor(out=xs(e, t), in0=tmp[:, t, :], scalar=m.gains[:, 0:1], in1=xs(e, t),
                                             op0=ALU.mult, op1=ALU.add).then_inc(s_x1, 1)

            def hidden(e, f):
                r = P if f < NF - 1 else FTAIL
                dve.wait_ge(s_silu, e * NF + f + 1)
                dve.tensor_tensor(hT[0:r, f, :], sg[0:r, f % 2, :], gps[0:r, f % 2, EW:2 * EW], ALU.mult).then_inc(s_h, 1)

            attn_result(0, 0, 0)
            residual1(0)
            moments(0, 0, s_x1)
            norm(0, 0, xn2)

            def residual2(e):
                for t in range(2):
                    dve.wait_ge(s_down, e * 2 + t + 1)
                    dve.scalar_tensor_tensor(out=xs(e, t), in0=dps[:, t, 0:D], scalar=m.gains[:, 2:3], in1=xs(e, t),
                                             op0=ALU.mult, op1=ALU.add).then_inc(s_x2, 1)

            def body(e, par, half, first, last):
                if not last:
                    if not first:
                        dve.wait_ge(s_attn, e * 2)
                    attn_result(e + 1, 1 - par, half + par)
                if not first:
                    residual2(e - 1)
                    moments(1, e - 1, s_x2)
                hidden(e, 0)
                if not first:
                    norm(1, e - 1, xn3)
                hidden(e, 1)
                if not last:
                    residual1(e + 1)
                hidden(e, 2)
                if not last:
                    moments(0, e + 1, s_x1)
                    dve.wait_ge(s_copy, e * 4 if not first else 2)
                    norm(0, e + 1, xn2)
                for f in range(3, NF):
                    hidden(e, f)

            experts(dve, body)
            residual2(E - 1)
            moments(1, E - 1, s_x2)
            norm(1, E - 1, xn3)

        @block.scalar
        def _(act):
            def copies(q, outs):
                for t in range(2):
                    act.wait_ge(s_turn, q + t + 1)
                    act.copy(outs[t], tps[:, t, 0:D].rearrange("p (k n) -> p k n", k=DK)).then_inc(s_copy, 1)

            def into_xn2T(par):
                return [xn2T[:, par, :, t * P:(t + 1) * P] for t in range(2)]

            def into_xnT(e):
                return [m.xnT[:, :, bass.ds(e * EW + t * P, P)] for t in range(2)]

            def silu(e, f):
                r = P if f < NF - 1 else FTAIL
                act.wait_ge(s_gu, e * NF + f + 1)
                act.wait_ge(s_h, e * NF + f + 1)
                act.activation(sg[0:r, f % 2, :], gps[0:r, f % 2, 0:EW], ACT.Silu).then_inc(s_silu, 1)

            copies(0, into_xn2T(0))

            def body(e, par, half, first, last):
                for f in range(3):
                    silu(e, f)
                if not first:
                    copies(e * 4, into_xnT(e - 1))
                for f in range(3, NF - 1):
                    silu(e, f)
                if not last:
                    copies(e * 4 + 2, into_xn2T(1 - par))
                silu(e, NF - 1)
                if last:
                    copies(e * 4 + 2, into_xnT(e))

            experts(act, body)

        @block.tensor
        def _(pe):
            def turn(q, i, n, src):
                for t in range(2):
                    pe.wait_ge(s_norm[i], n + t + 1)
                    pe.wait_ge(s_copy, q + t - 1 if not isinstance(q, int) or q >= 2 else 0)
                    for k in range(DK):
                        mm = pe.transpose(tps[:, t, k * P:(k + 1) * P], src[:, t, k * P:(k + 1) * P], m.ident[:, :])
                    mm.then_inc(s_turn, 1)

            def attn_out(e, par, first):
                pe.wait_ge(s_onorm, e + 1)
                for t in range(2):
                    if not first:
                        pe.wait_ge(s_bo, e * 2 + t - 1)
                    for k in range(DK):
                        mm = pe.matmul(aps[:, t, 0:D], on[:, par, k, t * P:(t + 1) * P], m.w0[:, WO * DK + k, :],
                                       start=(k == 0), stop=(k == DK - 1))
                    mm.then_inc(s_attn, 1)

            def gate_up(e, par, f):
                r = P if f < NF - 1 else FTAIL
                pe.wait_ge(s_h, e * NF + f + 1)
                for g in range(2):
                    for k in range(DK):
                        mm = pe.matmul(gps[0:r, f % 2, g * EW:(g + 1) * EW], w13[par][:, g * DK + k, f * P:f * P + r],
                                       xn2T[:, par, k, :], start=(k == 0), stop=(k == DK - 1))
                mm.then_inc(s_gu, 1)

            attn_out(0, 0, True)
            turn(0, 0, 0, xn2)

            def body(e, par, half, first, last):
                pe.wait_ge(s_w[par], half * 16 + 16)
                pe.wait_ge(s_copy, e * 4 if not first else 2)
                for f in range(2):
                    gate_up(e, par, f)
                if not last:
                    attn_out(e + 1, 1 - par, False)
                gate_up(e, par, 2)
                if not first:
                    turn(e * 4, 1, e * 2 - 2, xn3)
                for f in range(3, NF - 1):
                    gate_up(e, par, f)
                if not last:
                    turn(e * 4 + 2, 0, e * 2 + 2, xn2)
                gate_up(e, par, NF - 1)
                pe.wait_ge(s_h, e * NF + NF + 2)
                for t in range(2):
                    pe.wait_ge(s_x2, e * 2 + t + 1)
                    for f in range(NF):
                        r = P if f < NF - 1 else FTAIL
                        mm = pe.matmul(dps[:, t, 0:D], hT[0:r, f, t * P:(t + 1) * P], w2[par][0:r, f, :],
                                       start=(f == 0), stop=(f == NF - 1))
                    mm.then_inc(s_down, 1)
                if last:
                    turn(e * 4 + 2, 1, e * 2, xn3)

            experts(pe, body)


def phase5(nc, m):
    at = 0
    m.ks, at = region(m.reg_a, at, [P, DK, S])
    m.vs, at = region(m.reg_a, at, [P, NS, D])
    m.free_a = at
    m.kc, at = region(m.reg_f, 0, [P, DK, T])
    m.vc, at = region(m.reg_f, at, [P, NT, D])
    with ExitStack() as ctx:
        def sem(name):
            return ctx.enter_context(nc.semaphore("p5_" + name))

        kps = ctx.enter_context(nc.psum_tensor("p5_k", [P, 2, 512], F32))
        vps = ctx.enter_context(nc.psum_tensor("p5_v", [P, 2, 512], F32))
        s_back, s_k, s_kread, s_v, s_vread = (sem(n) for n in ("back", "k", "kread", "v", "vread"))
        block = ctx.enter_context(nc.Block())

        @block.sync
        def _(sp):
            sp.dma_start(m.ks, m.ks_keep).then_inc(s_back, 16)
            sp.dma_start(m.vs, m.vs_keep).then_inc(s_back, 16)
            sp.wait_ge(s_back, 32)

        @block.scalar
        def _(act):
            for n in range(8):
                mt, tb = n % 2, n // 2
                act.wait_ge(s_k, n + 1)
                act.activation(m.kc[:, mt, tb * 512:(tb + 1) * 512], kps[:, n % 2, :], ACT.Identity,
                               bias=m.cols[:, CBKC, mt:mt + 1]).then_inc(s_kread, 1)

        @block.vector
        def _(dve):
            for t in range(NT):
                dve.wait_ge(s_v, t + 1)
                dve.tensor_tensor(m.vc[:, t, :], vps[:, t % 2, 0:D], m.rows[:, RBVC, :], ALU.add).then_inc(s_vread, 1)

        @block.tensor
        def _(pe):
            for n in range(8):
                mt, tb = n % 2, n // 2
                if n >= 2:
                    pe.wait_ge(s_kread, n - 1)
                for k in range(DK):
                    mm = pe.matmul(kps[:, n % 2, :], m.w1[:, KC * DK + k, mt * P:(mt + 1) * P],
                                   m.xnT[:, k, tb * 512:(tb + 1) * 512], start=(k == 0), stop=(k == DK - 1))
                mm.then_inc(s_k, 1)
                for t in (2 * n, 2 * n + 1):
                    if t >= 2:
                        pe.wait_ge(s_vread, t - 1)
                    for k in range(DK):
                        mm = pe.matmul(vps[:, t % 2, 0:D], m.xnT[:, k, t * P:(t + 1) * P], m.w1[:, VC * DK + k, :],
                                       start=(k == 0), stop=(k == DK - 1))
                    mm.then_inc(s_v, 1)


def attention1(nc, m, side, ntile, nkey, nkt):
    tok = side == "tok"
    kT, v, keep = (m.ks, m.vs, m.c2s) if tok else (m.kc, m.vc, m.s2c)
    with ExitStack() as ctx:
        def sem(name):
            return ctx.enter_context(nc.semaphore(f"{side}_{name}"))

        def ps(name, n):
            return ctx.enter_context(nc.psum_tensor(f"{side}_{name}", [P, n, 512], F32))

        def small(name, shape):
            return ctx.enter_context(nc.sbuf_tensor(f"{side}_{name}", shape, F32))

        sps, tps, ops, qps = ps("scores", 4), ps("turn", 2), ps("out", 1), ps("q", 1)
        at = m.free_a
        prob, at = region(m.reg_a, at, [P, 2, NT * P])
        pT, at = region(m.reg_a, at, [P, NT, P])
        qb, at = region(m.reg_a, at, [P, 2, DK, P])
        ob, at = region(m.reg_a, at, [P, 2, D])
        mx, nm, total, rec = (small(n, [P, 2]) for n in ("mx", "nm", "total", "rec"))

        s_q, s_scores, s_mx, s_nm, s_exp, s_turn, s_pv, s_rec, s_o = (
            sem(n) for n in ("q", "scores", "mx", "nm", "exp", "turn", "pv", "rec", "o"))
        s_qproj = sem("qproj")
        s_pc = [sem(f"pc{i}") for i in range(2)]
        s_qload = [sem(f"qload{i}") for i in range(2)]
        s_store = [sem(f"store{i}") for i in range(2)]
        groups = [range(4 * j, min(4 * j + 4, nkt)) for j in range(4)]
        chunks = [(c * 512, min(512, nkey - c * 512)) for c in range(4)]

        def width(kt):
            return min(P, nkey - kt * P)

        def tiles(eng, body):
            body(0, 0, 0, True, False)
            with eng.Fori(0, (ntile - 1) // 2) as i:
                body(i * 2 + 1, 1, i, False, False)
                body(i * 2 + 2, 0, i + 1, False, ntile % 2 == 1 and None)
            if ntile % 2 == 0:
                body(ntile - 1, 1, ntile // 2 - 1, False, True)

        LAST = ntile - 1
        LPAR = LAST % 2

        block = ctx.enter_context(nc.Block())

        @block.sync
        def _(sp):
            def load(t, par):
                sp.dma_start(qb[:, par, :, :], m.qs_keep[bass.ds(t * P, P), :].rearrange("p (k n) -> p k n", k=DK)
                             ).then_inc(s_qload[par], 16)

            def store(t, par):
                sp.wait_ge(s_o, t + 2)
                sp.dma_start(keep[bass.ds(t * P, P), :], ob[:, par, :]).then_inc(s_store[par], 16)

            def body(t, par, half, first, last):
                if not tok:
                    if not first:
                        sp.wait_ge(s_scores, t)
                    load(t, par)
                if not first:
                    store(t - 1, 1 - par)

            for i in range(2):
                sp.sem_inc(s_store[i], 16)
            tiles(sp, body)
            store(LAST, LPAR)
            sp.wait_ge(s_store[0], 16 * (-(-ntile // 2) + 1))
            sp.wait_ge(s_store[1], 16 * (ntile // 2 + 1))

        @block.vector
        def _(dve):
            def copy_group(t, j):
                w = sum(width(kt) for kt in groups[j])
                n = len(groups[j])
                dve.wait_ge(s_turn, t * 4 + j + 1)
                if w == n * P:
                    src, dst = tps[:, j % 2, 0:w], flat(pT[:, 4 * j:4 * j + n, :])
                else:
                    src, dst = tps[0:w, j % 2, 0:P], pT[0:w, 4 * j, :]
                dve.tensor_copy(dst, src).then_inc(s_pc[0], 1)

            def maximum(t, par):
                dve.wait_ge(s_scores, t + 2)
                dve.tensor_reduce(mx[:, par:par + 1], flat(sps[:, :, :])[:, 0:nkey], AX.X, ALU.max).then_inc(s_mx, 1)
                dve.wait_ge(s_mx, t + 1)
                dve.tensor_scalar(nm[:, par:par + 1], mx[:, par:par + 1], -SC1, None, ALU.mult).then_inc(s_nm, 1)

            def finish(t, par, half):
                dve.wait_ge(s_exp, t + 1)
                dve.reciprocal(rec[:, par:par + 1], total[:, par:par + 1]).then_inc(s_rec, 1)
                dve.wait_ge(s_rec, t + 1)
                dve.wait_ge(s_pv, t + 1)
                dve.wait_ge(s_store[par], half * 16 + 16)
                dve.tensor_scalar(ob[:, par, :], ops[:, 0, 0:D], rec[:, par:par + 1], None, ALU.mult).then_inc(s_o, 1)

            def body(t, par, half, first, last):
                if not first:
                    copy_group(t - 1, 0)
                maximum(t, par)
                if not first:
                    copy_group(t - 1, 2)
                    finish(t - 1, 1 - par, half + par - 1 if par == 0 else half)

            dve.sem_inc(s_pc[0], 1)
            dve.sem_inc(s_o, 1)
            tiles(dve, body)
            copy_group(LAST, 0)
            copy_group(LAST, 2)
            finish(LAST, LPAR, LAST // 2)

        @block.scalar
        def _(act):
            def q_keep(t, par):
                act.wait_ge(s_qproj, t + 1)
                for mt in range(DK):
                    ins = act.activation(qb[:, par, mt, :], qps[:, 0, mt * P:(mt + 1) * P], ACT.Identity,
                                         bias=m.cols[:, CBQC, mt:mt + 1])
                ins.then_inc(s_q, 1)

            def copy_group(t, j):
                act.wait_ge(s_turn, t * 4 + j + 1)
                n = len(groups[j])
                w = width(groups[j][-1])
                if w == P:
                    src, dst = tps[:, j % 2, 0:n * P], flat(pT[:, 4 * j:4 * j + n, :])
                else:
                    src, dst = tps[0:w, j % 2, 0:P], pT[0:w, 4 * j, :]
                act.copy(dst, src).then_inc(s_pc[1], 1)

            def exps(t, par):
                act.wait_ge(s_nm, t + 1)
                act.activation(prob[:, par, 0:nkey], flat(sps[:, :, :])[:, 0:nkey], ACT.Exp, bias=nm[:, par:par + 1],
                               scale=SC1, accum_out=total[:, par:par + 1]).then_inc(s_exp, 1)

            if tok:
                q_keep(0, 0)

            def body(t, par, half, first, last):
                if tok and last is not True:
                    q_keep(t + 1, 1 - par)
                if not first:
                    copy_group(t - 1, 1)
                exps(t, par)
                if not first:
                    copy_group(t - 1, 3)

            act.sem_inc(s_pc[1], 1)
            tiles(act, body)
            copy_group(LAST, 1)
            copy_group(LAST, 3)

        @block.tensor
        def _(pe):
            def q_proj(t):
                pe.wait_ge(s_q, t)
                for mt in range(DK):
                    for k in range(DK):
                        mm = pe.matmul(qps[:, 0, mt * P:(mt + 1) * P], m.w1[:, QC * DK + k, mt * P:(mt + 1) * P],
                                       m.xnT[:, k, bass.ds(t * P, P)], start=(k == 0), stop=(k == DK - 1))
                mm.then_inc(s_qproj, 1)

            def scores(t, par, half, first):
                if tok:
                    pe.wait_ge(s_q, t + 1)
                else:
                    pe.wait_ge(s_qload[par], half * 16 + 16)
                if not first:
                    pe.wait_ge(s_exp, t)
                for c, (o, w) in enumerate(chunks):
                    for k in range(DK):
                        mm = pe.matmul(sps[:, c, 0:w], qb[:, par, k, :], kT[:, k, o:o + w],
                                       start=(k == 0), stop=(k == DK - 1))
                mm.then_inc(s_scores, 1)

            def turn_group(t, par, j):
                pe.wait_ge(s_pc[j % 2], t * 2 + j // 2 + 1)
                for i, kt in enumerate(groups[j]):
                    w = width(kt)
                    mm = pe.transpose(tps[0:w, j % 2, i * P:(i + 1) * P], prob[:, par, kt * P:kt * P + w], m.ident[:, :])
                mm.then_inc(s_turn, 1)

            def pv_group(t, j):
                pe.wait_ge(s_pc[j % 2], t * 2 + j // 2 + 2)
                for kt in groups[j]:
                    w = width(kt)
                    mm = pe.matmul(ops[:, 0, 0:D], pT[0:w, kt, :], v[0:w, kt, :], start=(kt == 0), stop=(kt == nkt - 1))
                return mm

            def values(t, par):
                pe.wait_ge(s_exp, t + 1)
                turn_group(t, par, 0)
                turn_group(t, par, 1)
                pe.wait_ge(s_o, t + 1)
                pv_group(t, 0)
                turn_group(t, par, 2)
                pv_group(t, 1)
                turn_group(t, par, 3)
                pv_group(t, 2)
                pv_group(t, 3).then_inc(s_pv, 1)

            pe.sem_inc(s_scores, 1)
            if tok:
                q_proj(0)

            def body(t, par, half, first, last):
                scores(t, par, half, first)
                if tok and last is not True:
                    q_proj(t + 1)
                if not first:
                    values(t - 1, 1 - par)

            tiles(pe, body)
            values(LAST, LPAR)


def phase8(nc, m):
    with ExitStack() as ctx:
        def sem(name):
            return ctx.enter_context(nc.semaphore("p8_" + name))

        def ps(name):
            return ctx.enter_context(nc.psum_tensor("p8_" + name, [P, 512], F32))

        def small(name, shape):
            return ctx.enter_context(nc.sbuf_tensor("p8_" + name, shape, F32))

        ips, cps, eps_, gps, xps, yps = (ps(n) for n in ("stretch", "turn_c", "turn_s", "gate", "turn_x", "filter"))
        at = 0
        stretch, at = region(m.reg_a, at, [P, 2, P])
        win, at = region(m.reg_a, at, [P, 2, D])
        cb, at = region(m.reg_a, at, [P, 2, D])
        sbuf, at = region(m.reg_a, at, [P, 2, D])
        gT, at = region(m.reg_a, at, [P, 2, 2 * DK, P])
        gb, at = region(m.reg_a, at, [P, D])
        gate, at = region(m.reg_a, at, [P, D])
        dif, at = region(m.reg_a, at, [P, D])
        mul, at = region(m.reg_a, at, [P, D])
        mix, at = region(m.reg_a, at, [P, D])
        xn, at = region(m.reg_a, at, [P, D])
        xT, at = region(m.reg_a, at, [P, DK, P])
        yb, at = region(m.reg_a, at, [P, D])
        ob, at = region(m.reg_a, at, [P, 2, D])
        st, mv, var, rstd = small("st", [P, 6]), small("mv", [P, 2]), small("var", [P, 1]), small("rstd", [P, 1])

        s_passed = sem("passed")
        s_in = [sem(f"in{i}") for i in range(2)]
        s_store = [sem(f"store{i}") for i in range(2)]
        s_stretch, s_scopy, s_tc, s_tccopy, s_ts, s_tscopy, s_gate, s_gb, s_sig = (
            sem(n) for n in ("stretch", "scopy", "tc", "tccopy", "ts", "tscopy", "gate", "gb", "sig"))
        s_dif, s_mul, s_mix, s_x3, s_st, s_mv, s_var, s_rstd, s_norm = (
            sem(n) for n in ("dif", "mul", "mix", "x3", "st", "mv", "var", "rstd", "norm"))
        s_tx, s_txcopy, s_y, s_yb, s_out = (sem(n) for n in ("tx", "txcopy", "y", "yb", "out"))

        def tiles(eng, body):
            body(0, 0, 0, (True, False, False))
            body(1, 1, 0, (True, True, False))
            with eng.Fori(0, NT // 2 - 1) as i:
                body(i * 2 + 2, 0, i + 1, (True, True, True))
                body(i * 2 + 3, 1, i + 1, (True, True, True))
            body(NT, 0, NT // 2, (False, True, True))
            body(NT + 1, 1, NT // 2, (False, False, True))

        def xs(t):
            return m.x[:, bass.ds(t, 1), :].rearrange("p o d -> p (o d)")

        block = ctx.enter_context(nc.Block())

        @block.sync
        def _(sp):
            def body(t, par, half, run):
                if run[0]:
                    if not (isinstance(t, int) and t < 2):
                        sp.wait_ge(s_mix, t - 1)
                        sp.wait_ge(s_tc, t - 1)
                    sp.dma_start(stretch[:, par, :], m.interp[bass.ds(t * P, P), :]).then_inc(s_in[par], 16)
                    sp.dma_start(win[:, par, :], m.s2c[bass.ds(t * STRIDE, P), :]).then_inc(s_in[par], 16)
                    sp.dma_start(cb[:, par, :], m.c2s[bass.ds(t * P, P), :]).then_inc(s_in[par], 16)
                if run[2]:
                    sp.wait_ge(s_out, t - 1)
                    sp.dma_start(m.out[bass.ds(t * P - 2 * P, P), :], ob[:, par, :]).then_inc(s_store[par], 16)

            for i in range(2):
                sp.sem_inc(s_store[i], 16)
            tiles(sp, body)
            for i in range(2):
                sp.wait_ge(s_store[i], 16 * NT // 2 + 16)

        @block.gpsimd
        def _(pool):
            def body(t, par, half, run):
                if run[1]:
                    pool.wait_ge(s_var, t)
                    pool.tensor_tensor(rstd[:, :], var[:, :], m.neghalf[:, 0:1], ALU.pow).then_inc(s_rstd, 1)

            tiles(pool, body)

        @block.vector
        def _(dve):
            def body(t, par, half, run):
                if run[2]:
                    dve.wait_ge(s_y, t - 1)
                    dve.tensor_tensor(yb, yps[:, 0:D], m.rows[:, RBF, :], ALU.add).then_inc(s_yb, 1)
                    dve.wait_ge(s_yb, t)
                    dve.wait_ge(s_store[par], half * 16)
                    dve.scalar_tensor_tensor(out=ob[:, par, :], in0=yb, scalar=m.gains[:, 3:4], in1=xs(t - 2),
                                             op0=ALU.mult, op1=ALU.add).then_inc(s_out, 1)
                if run[1]:
                    q = 1 - par
                    dve.wait_ge(s_gate, t)
                    dve.tensor_tensor(gb, gps[:, 0:D], m.rows[:, RBG, :], ALU.add).then_inc(s_gb, 1)
                    dve.tensor_tensor(dif, cb[:, q, :], sbuf[:, q, :], ALU.subtract).then_inc(s_dif, 1)
                    dve.wait_ge(s_dif, t)
                    dve.wait_ge(s_sig, t)
                    dve.tensor_tensor(mul, gate, dif, ALU.mult).then_inc(s_mul, 1)
                    dve.wait_ge(s_mul, t)
                    dve.tensor_tensor(mix, mul, sbuf[:, q, :], ALU.add).then_inc(s_mix, 1)
                    dve.wait_ge(s_mix, t)
                    dve.scalar_tensor_tensor(out=xs(t - 1), in0=mix, scalar=m.gains[:, 1:2], in1=xs(t - 1),
                                             op0=ALU.mult, op1=ALU.add).then_inc(s_x3, 1)
                    wait_apart(dve, s_x3, t, s_passed)
                    dve.bn_stats(st[:, :], xs(t - 1)).then_inc(s_st, 1)
                    wait_apart(dve, s_st, t, s_passed)
                    dve.bn_aggr(mv[:, :], st[:, :]).then_inc(s_mv, 1)
                    dve.wait_ge(s_mv, t)
                    dve.tensor_scalar(var[:, :], mv[:, 1:2], EPS, None, ALU.add).then_inc(s_var, 1)
                    dve.wait_ge(s_rstd, t)
                    dve.wait_ge(s_tx, t - 1)
                    dve.tensor_scalar(xn, xs(t - 1), mv[:, 0:1], rstd[:, :], ALU.subtract, ALU.mult).then_inc(s_norm, 1)

            dve.sem_inc(s_yb, 1)
            tiles(dve, body)

        @block.scalar
        def _(act):
            def halves(a):
                return a[:, 0:D].rearrange("p (k n) -> p k n", k=DK)

            def body(t, par, half, run):
                if run[0]:
                    act.wait_ge(s_stretch, t + 1)
                    if not (isinstance(t, int) and t < 2):
                        act.wait_ge(s_mix, t - 1)
                    act.copy(sbuf[:, par, :], ips[:, 0:D]).then_inc(s_scopy, 1)
                    act.wait_ge(s_tc, t + 1)
                    act.copy(gT[:, par, 0:DK, :], halves(cps)).then_inc(s_tccopy, 1)
                if run[2]:
                    act.wait_ge(s_tx, t - 1)
                    act.copy(xT, halves(xps)).then_inc(s_txcopy, 1)
                if run[0]:
                    act.wait_ge(s_ts, t + 1)
                    act.copy(gT[:, par, DK:, :], halves(eps_)).then_inc(s_tscopy, 1)
                if run[1]:
                    act.wait_ge(s_gb, t)
                    act.activation(gate, gb, ACT.Sigmoid).then_inc(s_sig, 1)

            act.sem_inc(s_txcopy, 1)
            tiles(act, body)

        @block.tensor
        def _(pe):
            def body(t, par, half, run):
                if run[0]:
                    pe.wait_ge(s_in[par], half * 48 + 48)
                    pe.wait_ge(s_scopy, t)
                    pe.matmul(ips[:, 0:D], stretch[:, par, :], win[:, par, :], start=True, stop=True).then_inc(s_stretch, 1)
                    pe.wait_ge(s_tccopy, t)
                    for k in range(DK):
                        mm = pe.transpose(cps[:, k * P:(k + 1) * P], cb[:, par, k * P:(k + 1) * P], m.ident[:, :])
                    mm.then_inc(s_tc, 1)
                if run[2]:
                    pe.wait_ge(s_norm, t - 1)
                    pe.wait_ge(s_txcopy, t - 1)
                    for k in range(DK):
                        mm = pe.transpose(xps[:, k * P:(k + 1) * P], xn[:, k * P:(k + 1) * P], m.ident[:, :])
                    mm.then_inc(s_tx, 1)
                if run[1]:
                    pe.wait_ge(s_tscopy, t)
                    pe.wait_ge(s_gb, t - 1)
                    for k in range(2 * DK):
                        mm = pe.matmul(gps[:, 0:D], gT[:, 1 - par, k, :], m.w1[:, 6 * DK + k, :],
                                       start=(k == 0), stop=(k == 2 * DK - 1))
                    mm.then_inc(s_gate, 1)
                if run[0]:
                    pe.wait_ge(s_scopy, t + 1)
                    for k in range(DK):
                        mm = pe.transpose(eps_[:, k * P:(k + 1) * P], sbuf[:, par, k * P:(k + 1) * P], m.ident[:, :])
                    mm.then_inc(s_ts, 1)
                if run[2]:
                    pe.wait_ge(s_txcopy, t)
                    pe.wait_ge(s_yb, t - 1)
                    for k in range(DK):
                        mm = pe.matmul(yps[:, 0:D], xT[:, k, :], m.filt[:, k, :], start=(k == 0), stop=(k == DK - 1))
                    mm.then_inc(s_y, 1)

            tiles(pe, body)


STRIDE = 99


def kernel(**inputs):
    import numpy as np
    import concourse.bacc as bacc
    from concourse.bass_utils import run_bass_kernel_spmd

    a = {k: np.asarray(v) for k, v in inputs.items()}

    def tiled(w):
        return w.reshape(-1, P, w.shape[-1]).transpose(1, 0, 2)

    def by_group(w):
        return w.reshape(-1, H // G, G, HD).transpose(0, 1, 3, 2).reshape(w.shape)

    l0 = [by_group(a["L0_xattn_Wq"]), by_group(a["L0_xattn_Wk"]), a["L0_xattn_Wv"], a["L0_xattn_Wo"]]
    l1 = [a["L1_xattn_W" + n].T for n in ("q_c", "k_s", "v_s", "q_s", "k_c", "v_c", "g")]
    cols = [by_group(a["L0_xattn_b" + n]) for n in "qk"]
    cols += [a[n] for n in ("L1_xattn_bk_s", "L1_xattn_bq_s", "L1_xattn_bk_c", "L1_xattn_bq_c")]
    rows = [a[n] for n in ("L0_xattn_bv", "L0_xattn_bo", "L1_xattn_bv_s", "L1_xattn_bv_c", "L1_xattn_bg", "L1_ffn_bias")]
    ctx_T = np.zeros((P, DK, SP_), np.float32)
    ctx_T[:, :, :S] = tiled(a["ctx_1024"][0].T)
    w13 = [a["L0_ffn_" + n].reshape(E, DK, P, F).transpose(0, 2, 1, 3).reshape(E * P, DK * F) for n in ("w1", "w3")]
    w2 = np.zeros((E, NF * P, D), np.float32)
    w2[:, :F] = a["L0_ffn_w2"]
    w2 = w2.reshape(E, NF, P, D).transpose(0, 2, 1, 3).reshape(E * P, NF * D)

    n = np.arange(D)
    angle = 2 * np.pi * ((n[:, None] * n[None, :]) % D) / D
    cos, sin = np.cos(angle), np.sin(angle)
    dft = np.concatenate([tiled(x.astype(np.float32)) for x in (cos, sin, cos / D, sin / D, -sin / D)], axis=1)

    pos = (np.arange(T, dtype=np.float32) + np.float32(0.5)) * np.float32(S / T) - np.float32(0.5)
    pos = np.clip(pos, np.float32(0), np.float32(S - 1))
    lo = np.floor(pos).astype(np.int64)
    hi = np.minimum(lo + 1, S - 1)
    frac = pos - lo.astype(np.float32)
    interp = np.zeros((NT, P, P), np.float32)
    for j in range(T):
        t = j // P
        assert STRIDE * t <= lo[j] and hi[j] < STRIDE * t + P
        interp[t, lo[j] - STRIDE * t, j % P] += np.float32(1) - frac[j]
        interp[t, hi[j] - STRIDE * t, j % P] += frac[j]

    data = {
        "x_in": a["x"][0],
        "ctx_T": ctx_T,
        "w_l0": np.concatenate([tiled(w) for w in l0], axis=1),
        "w_l1": np.concatenate([tiled(w) for w in l1], axis=1),
        "b_cols": np.stack([b.reshape(DK, P).T for b in cols], axis=1),
        "b_rows": np.stack(rows)[None],
        "g_in": np.concatenate([a["g_xattn"], a["g_ffn"]])[None],
        "w_exp": np.concatenate([*w13, w2], axis=1),
        "wf_T": np.concatenate([tiled(a["L1_ffn_w_freq_" + k].T) for k in ("real", "imag")], axis=1),
        "eye": np.eye(P, dtype=np.float32),
        "dft": dft,
        "interp": interp.reshape(NT * P, P),
    }
    nc = bacc.Bacc("TRN2", target_bir_lowering=False, num_devices=1)
    arrays, aps = {}, {}
    for name, x in data.items():
        arrays[name] = np.ascontiguousarray(x)
        aps[name] = nc.dram_tensor(name, x.shape, mybir.dt.from_np(x.dtype), kind="ExternalInput").ap()
    aps["out"] = nc.dram_tensor("out", (T, D), F32, kind="ExternalOutput").ap()
    build(nc, aps)
    r = run_bass_kernel_spmd(nc, [arrays], core_ids=[0])
    return r.results[0]["out"].reshape(1, T, D)
```

```python
from contextlib import ExitStack

import concourse.bass as bass
from concourse import mybir

F32 = mybir.dt.float32
BF16 = mybir.dt.bfloat16
ALU = mybir.AluOpType
ACT = mybir.ActivationFunctionType
AX = mybir.AxisListType

P = 128
T = 2048
D = 256
DK = D // P
S = 1601
NT = T // P
NS = -(-S // P)
SP_ = NS * P
STAIL = S - (NS - 1) * P
H = 16
HD = D // H
E = 8
EW = T // E
F = 704
NF = -(-F // P)
FTAIL = F - (NF - 1) * P
EPS = 1e-5
SC0 = HD ** -0.5
SC1 = D ** -0.5

G = 4
QW = T // 2
NB = 2 * (H // G)
TERMS = [(0, 3, 0), (1, 2, 3 * HD), (2, 1, 5 * HD)]
NROW = 6 * HD
MROW = 3
CW = 401
CSTEP = 400
NCH = G * (QW // P) * 2

WQ, WK, WV, WO = range(4)
QC, KS, VS, QS, KC, VC = range(6)
CBQ, CBK, CBKS, CBQS, CBKC, CBQC = range(6)
RBV, RBO, RBVS, RBVC, RBG, RBF = range(6)


class Tensors:
    pass


def flat(ap):
    return ap.rearrange("p a b -> p (a b)")


def build(nc, A):
    with ExitStack() as ctx:
        def sb(name, shape, dt=F32):
            return ctx.enter_context(nc.sbuf_tensor(name, shape, dt))

        def dram(name, shape, dt=F32):
            return nc.dram_tensor(name, shape, dt, kind="Internal").ap()

        m = Tensors()
        m.x_in, m.ctx_T, m.out = A["x_in"], A["ctx_T"], A["out"]
        m.w_l0, m.w_l1, m.w_exp, m.wf_T = A["w_l0"], A["w_l1"], A["w_exp"], A["wf_T"]
        m.b_cols, m.b_rows, m.g_in = A["b_cols"], A["b_rows"], A["g_in"]
        m.eye, m.dft, m.interp = A["eye"], A["dft"], A["interp"]
        m.q_parts = dram("q_parts", (3, 2 * D, QW), BF16)
        m.k_parts = dram("k_parts", (3, D, SP_), BF16)
        m.v_blocks = dram("v_blocks", (H // G * P, NS * P))
        m.o_all = dram("o_all", (2, 2 * D, QW))
        m.ks_keep = dram("ks_keep", (P, DK, S))
        m.vs_keep = dram("vs_keep", (P, NS, D))
        m.qs_keep = dram("qs_keep", (NS * P, DK * P))
        m.c2s = dram("c2s", (T, D))
        m.s2c = dram("s2c", (SP_, D))

        m.x = sb("x_rows", [P, NT, D])
        m.w0 = sb("w_layer0", [P, 4 * DK, D])
        m.w1 = sb("w_layer1", [P, 6 * DK + 4, D])
        m.filt = sb("filter_matrix", [P, DK, D])
        m.rows = sb("bias_rows", [P, 6, D])
        m.cols = sb("bias_cols", [P, 6, DK])
        m.bq_scaled = sb("bq_scaled", [P, DK])
        m.gains = sb("gains", [P, 4])
        m.ident = sb("ident", [P, P])
        m.ident_b = sb("ident_b", [P, P], BF16)
        m.xnT = sb("xn_T", [P, DK, T])
        m.neghalf = sb("neghalf", [P, NT])
        m.warm = sb("table_warm_up", [P, 1])
        m.passed = ctx.enter_context(nc.semaphore("passed"))

        m.reg_f = sb("region_f", [P, 2 * (2 * DK * F + NF * D)])
        m.reg_a = sb("region_a", [P, 23296])
        at = [0]

        def attn(n, shape, dt=F32):
            size = n // 2 if dt == BF16 else n
            v = m.reg_a[:, at[0]:at[0] + size]
            at[0] += size
            return v.bitcast(dt) if dt == BF16 else v

        m.kst, m.qst, m.vb = [], [], []
        for _ in range(2):
            m.kst.append(attn(G * SP_, None, BF16).rearrange("p (h n) -> p h n", h=G))
            m.qst.append(attn(G * QW, None, BF16).rearrange("p (h n) -> p h n", h=G))
            m.vb.append(attn(NS * P, None).rearrange("p (k n) -> p k n", k=NS))
        m.prob = [attn(G * QW, None).rearrange("p (h n) -> p h n", h=G) for _ in range(2)]
        m.oT = attn(QW, None).rearrange("p (b n) -> p b n", b=2)
        m.mx = sb("chunk_maxima", [P, NCH])
        m.mx1 = sb("maxima", [P, NCH // 2])
        m.mrest = sb("maxima_rest", [P, NCH // 2])
        m.mparts = sb("maxima_parts", [P, MROW, NCH // 2], BF16)
        m.mT = sb("maxima_rows", [P, P], BF16)

        phase1(nc, m)
        phase2(nc, m)
        phase3(nc, m)
        phase4(nc, m)
        phase5(nc, m)
        attention1(nc, m, "tok", NT, S, NS)
        attention1(nc, m, "ctx", NS, T, NT)
        phase8(nc, m)


def wait_apart(eng, sem, value, passed):
    eng.wait_ge(sem, value)
    eng.sem_inc(passed, 1)


def warm_up(act, m, function):
    act.activation(m.warm[:, :], m.gains[:, 0:1], function)


def region(base, at, shape):
    n = 1
    for s in shape[1:]:
        n *= s
    v = base[:, at:at + n]
    if len(shape) == 3:
        v = v.rearrange("p (a b) -> p a b", b=shape[2])
    elif len(shape) == 4:
        v = v.rearrange("p (a b c) -> p a b c", b=shape[2], c=shape[3])
    return v, at + n


def phase1(nc, m):
    with ExitStack() as ctx:
        def sem(name):
            return ctx.enter_context(nc.semaphore("p1_" + name))

        def ps(name, shape, dt=F32):
            return ctx.enter_context(nc.psum_tensor("p1_" + name, shape, dt))

        proj = ps("proj", [P, 3, 512])
        vps = ps("vps", [P, 2, 512])
        tps = ps("tps", [P, 2, 512])
        ctxT, _ = region(m.reg_f, 0, [P, DK, SP_])
        base = m.reg_a
        a0 = (G * SP_ + G * QW) // 2 + NS * P
        xf, a0 = region(base, a0, [P, 2, 512])
        r1, a0 = region(base, a0, [P, 2, 512])
        NPB = 4
        parts = base[:, a0:a0 + NPB * 3 * 256].bitcast(BF16).rearrange("p (s a n) -> p s a n", s=NPB, a=3)
        a0 = 2 * ((G * SP_ + G * QW) // 2 + NS * P)
        vaug, a0 = region(base, a0, [P, NS, H, 32])
        m.vaug = vaug
        xn, a0 = region(base, 2 * ((G * SP_ + G * QW) // 2 + NS * P) + 2 * G * QW, [P, 2, D])
        stats = ctx.enter_context(nc.sbuf_tensor("p1_stats", [P, NT, 6], F32))
        mv = ctx.enter_context(nc.sbuf_tensor("p1_mv", [P, NT, 2], F32))
        var = ctx.enter_context(nc.sbuf_tensor("p1_var", [P, NT], F32))
        rstd = ctx.enter_context(nc.sbuf_tensor("p1_rstd", [P, NT], F32))
        gin = ctx.enter_context(nc.sbuf_tensor("p1_gin", [P, 4], F32))

        s_ctx, s_w0, s_cols, s_x, s_rows, s_ident, s_late, s_gin = (
            sem(n) for n in ("ctx", "w0", "cols", "x", "rows", "ident", "late", "gin"))
        s_bq, s_stats, s_aggr, s_var, s_rstd, s_norm = (
            sem(n) for n in ("bq", "stats", "aggr", "var", "rstd", "norm"))
        s_xT, s_xTcopy, s_proj, s_p1, s_r1, s_p2, s_p3 = (
            sem(n) for n in ("xT", "xTcopy", "proj", "p1", "r1", "p2", "p3"))
        s_vproj, s_vbias, s_const = (sem(n) for n in ("vproj", "vbias", "const"))
        s_kload = sem("kload")
        s_pout = [sem(f"pout{i}") for i in range(NPB)]

        def chunk(g):
            if g < 8:
                return WK, g // 4, (g % 4) * 512, min(512, S - (g % 4) * 512)
            return WQ, g % 2, ((g - 8) // 2) * 512, 512

        def v_tiles(g):
            return range(2 * (g - 8), min(2 * (g - 8) + 2, NS))

        def stored(g):
            return 16 * sum(1 if c < 8 else 2 for c in range(g % NPB, g, NPB))

        block = ctx.enter_context(nc.Block())

        @block.sync
        def _(sp):
            sp.dma_start(m.x[:, :, :], m.x_in.rearrange("(t p) d -> p t d", p=P)).then_inc(s_x, 16)
            sp.dma_start(m.cols[:, :, :], m.b_cols).then_inc(s_cols, 16)
            sp.dma_start(ctxT, m.ctx_T).then_inc(s_ctx, 16)
            sp.dma_start(m.w0[:, :, :], m.w_l0).then_inc(s_w0, 16)
            sp.dma_start(m.ident[:, :], m.eye).then_inc(s_ident, 16)
            sp.dma_start(m.rows[:, :, :], m.b_rows.to_broadcast([P, 6, D])).then_inc(s_rows, 16)
            sp.dma_start(gin[:, :], m.g_in.to_broadcast([P, 4])).then_inc(s_gin, 16)
            sp.dma_start(m.w1[:, :, :], m.w_l1).then_inc(s_late, 16)
            for g in range(16):
                _, mt, col, w = chunk(g)
                sp.wait_ge(s_p3, g + 1)
                src = parts[:, g % NPB, :, 0:w]
                if g < 8:
                    w = min(512, SP_ - col)
                    dst = m.k_parts.rearrange("a r n -> r a n")[mt * P:mt * P + P, :, col:col + w]
                    sp.dma_start(dst, parts[:, g % NPB, :, 0:w]).then_inc(s_pout[g % NPB], 16)
                else:
                    for c in range(2):
                        r = c * D + mt * P
                        dst = m.q_parts.rearrange("a r n -> r a n")[r:r + P, :, col // 2:col // 2 + EW]
                        sp.dma_start(dst, src[:, :, c * EW:(c + 1) * EW]).then_inc(s_pout[g % NPB], 16)
                if g == 7:
                    for n in range(NPB):
                        sp.wait_ge(s_pout[n], stored(8 + n))
                    load_k(sp, m, 0, 0, s_kload)
            for n in range(NPB):
                sp.wait_ge(s_pout[n], stored(16 + n))
            sp.wait_ge(s_kload, 16 * len(TERMS))
            sp.wait_ge(s_late, 16)

        @block.gpsimd
        def _(pool):
            pool.memset(vaug[:, :, :, 0:HD], 0.0).then_inc(s_const, 1)
            pool.memset(vaug[:, 0:NS - 1, :, HD:], 1.0).then_inc(s_const, 1)
            pool.memset(vaug[:, NS - 1, :, HD:], 0.0).then_inc(s_const, 1)
            pool.wait_ge(s_const, 3)
            pool.memset(vaug[0:STAIL, NS - 1, :, HD:], 1.0).then_inc(s_const, 1)
            pool.memset(m.neghalf[:, :], -0.5).then_inc(s_const, 1)
            pool.wait_ge(s_const, 5)
            pool.wait_ge(s_var, 1)
            pool.tensor_tensor(rstd[:, :], var[:, :], m.neghalf[:, :], ALU.pow).then_inc(s_rstd, 1)
            pool.wait_ge(s_rstd, 1)
            ones_rows(pool, m, 0, s_const, 5)
            pool.wait_ge(s_const, 7)

        @block.vector
        def _(dve):
            dve.wait_ge(s_cols, 16)
            dve.tensor_scalar(m.bq_scaled[:, :], m.cols[:, CBQ, :], SC0, None, ALU.mult).then_inc(s_bq, 1)
            dve.wait_ge(s_x, 16)
            for t in range(NT):
                dve.bn_stats(stats[:, t, :], m.x[:, t, :]).then_inc(s_stats, 1)
            for t in range(NT):
                dve.wait_ge(s_stats, t + 1)
                dve.bn_aggr(mv[:, t, :], stats[:, t, :]).then_inc(s_aggr, 1)
            dve.wait_ge(s_aggr, NT)
            dve.tensor_scalar(var[:, :], mv[:, :, 1], EPS, None, ALU.add).then_inc(s_var, 1)
            dve.wait_ge(s_ident, 16)
            dve.tensor_copy(m.ident_b[:, :], m.ident[:, :])

            def norm(t):
                if t == 0:
                    dve.wait_ge(s_rstd, 1)
                if t >= 2:
                    dve.wait_ge(s_xT, t - 1)
                dve.tensor_scalar(xn[:, t % 2, :], m.x[:, t, :], mv[:, t, 0:1], rstd[:, t:t + 1],
                                  ALU.subtract, ALU.mult).then_inc(s_norm, 1)

            def split(g):
                w = chunk(g)[3]
                p = parts[:, g % NPB, :, 0:w]
                dve.wait_ge(s_p1, g + 1)
                if g < 8 and w == STAIL:
                    dve.memset(parts[:, g % NPB, :, w:P], 0.0)
                dve.tensor_tensor(r1[:, g % 2, 0:w], xf[:, g % 2, 0:w], p[:, 0, :], ALU.subtract).then_inc(s_r1, 1)
                dve.wait_ge(s_r1, g + 1)
                dve.tensor_copy(p[:, 1, :], r1[:, g % 2, 0:w]).then_inc(s_p2, 1)
                dve.wait_ge(s_p2, g + 1)
                dve.tensor_tensor(p[:, 2, :], r1[:, g % 2, 0:w], p[:, 1, :], ALU.subtract).then_inc(s_p3, 1)

            for n in range(8):
                norm(2 * n)
                norm(2 * n + 1)
                split(n)
            dve.wait_ge(s_rows, 16)
            dve.wait_ge(s_const, 4)
            for g in range(8, 16):
                split(g)
                for kt in v_tiles(g):
                    r = P if kt < NS - 1 else STAIL
                    dve.wait_ge(s_vproj, kt + 1)
                    dve.tensor_tensor(vaug[0:r, kt, :, 0:HD],
                                      vps[0:r, kt % 2, 0:D].rearrange("p (h d) -> p h d", h=H),
                                      m.rows[0:r, RBV, :].rearrange("p (h d) -> p h d", h=H),
                                      ALU.add).then_inc(s_vbias, 1)

        @block.scalar
        def _(act):
            act.wait_ge(s_gin, 16)
            act.activation(m.gains[:, :], gin[:, :], ACT.Tanh)
            act.wait_ge(s_cols, 16)

            def values(g):
                which, mt, _, w = chunk(g)
                scale = SC0 if which == WQ else 1.0
                bias = m.bq_scaled[:, mt:mt + 1] if which == WQ else m.cols[:, CBK, mt:mt + 1]
                act.wait_ge(s_proj, g + 1)
                if g >= 2:
                    act.wait_ge(s_p3, g - 1)
                if g >= NPB:
                    act.wait_ge(s_pout[g % NPB], stored(g))
                act.activation(xf[:, g % 2, 0:w], proj[:, g % 3, 0:w], ACT.Identity, bias=bias, scale=scale)
                act.activation(parts[:, g % NPB, 0, 0:w], proj[:, g % 3, 0:w], ACT.Identity,
                               bias=bias, scale=scale).then_inc(s_p1, 1)

            def keep_xT(t):
                act.wait_ge(s_xT, t + 1)
                act.copy(m.xnT[:, :, t * P:(t + 1) * P],
                         tps[:, t % 2, 0:D].rearrange("p (k n) -> p k n", k=DK)).then_inc(s_xTcopy, 1)

            for n in range(8):
                values(n)
                keep_xT(2 * n)
                keep_xT(2 * n + 1)
            act.wait_ge(s_bq, 1)
            for g in range(8, 16):
                values(g)

        @block.tensor
        def _(pe):
            def project(g):
                which, mt, col, w = chunk(g)
                rhs = ctxT if which == WK else m.xnT
                if which == WQ:
                    pe.wait_ge(s_xTcopy, col // P + 4)
                if g >= 3:
                    pe.wait_ge(s_p1, g - 2)
                for k in range(DK):
                    mm = pe.matmul(proj[:, g % 3, 0:w], m.w0[:, which * DK + k, mt * P:(mt + 1) * P],
                                   rhs[:, k, col:col + w], start=(k == 0), stop=(k == DK - 1))
                mm.then_inc(s_proj, 1)

            def turn(t):
                pe.wait_ge(s_norm, t + 1)
                if t >= 2:
                    pe.wait_ge(s_xTcopy, t - 1)
                for k in range(DK):
                    mm = pe.transpose(tps[:, t % 2, k * P:(k + 1) * P], xn[:, t % 2, k * P:(k + 1) * P], m.ident[:, :])
                mm.then_inc(s_xT, 1)

            pe.wait_ge(s_ctx, 16)
            pe.wait_ge(s_w0, 16)
            for n in range(8):
                project(n)
                if n == 0:
                    pe.wait_ge(s_ident, 16)
                turn(2 * n)
                turn(2 * n + 1)
            for g in range(8, 16):
                project(g)
                for kt in v_tiles(g):
                    if kt >= 2:
                        pe.wait_ge(s_vbias, kt - 1)
                    for k in range(DK):
                        mm = pe.matmul(vps[:, kt % 2, 0:D], ctxT[:, k, kt * P:(kt + 1) * P], m.w0[:, WV * DK + k, :],
                                       start=(k == 0), stop=(k == DK - 1))
                    mm.then_inc(s_vproj, 1)


def ones_rows(pool, m, par, signal, base):
    pool.memset(m.kst[par][NROW:NROW + MROW, :, S:], 0.0).then_inc(signal, 1)
    pool.wait_ge(signal, base + 1)
    pool.memset(m.kst[par][NROW:NROW + MROW, :, 0:S], 1.0).then_inc(signal, 1)


def load_k(eng, m, i, par, signal):
    rows = m.k_parts[:, bass.ds(i * (G * HD), G * HD), :].rearrange("a (d h) n -> a d (h n)", h=G)
    for _, n, r in TERMS:
        eng.dma_start(flat(m.kst[par][r:r + n * HD, :, :]), rows[0:n]).then_inc(signal, 16)


def load_q(eng, m, i, par, signal):
    for a, n, r in TERMS:
        src = m.q_parts[a:a + 1, bass.ds(par * D + i * (G * HD), G * HD), :].rearrange("a (d h) n -> a d (h n)", h=G)
        eng.dma_start(flat(m.qst[par][r:r + n * HD, :, :]),
                      src.to_broadcast([n, HD, G * QW])).then_inc(signal, 16)


def load_v(eng, m, i, par, signal):
    eng.dma_start(m.vb[par], m.v_blocks[bass.ds(i * P, P), :].rearrange("p (k n) -> p k n", k=NS)).then_inc(signal, 16)


KQ_LOADS = 16 * 2 * len(TERMS)


def chunk_scores(pe, m, par, kpar, n, out, signal):
    h, qt, c = n // (2 * (QW // P)), n // 2 % (QW // P), n % 2
    for j in range(2):
        off = (2 * c + j) * CSTEP
        mm = pe.matmul(out[:, j, 0:CW], m.qst[par][0:NROW, h, qt * P:(qt + 1) * P],
                       m.kst[kpar][0:NROW, h, off:off + CW], start=True, stop=True)
    mm.then_inc(signal, 1)


def minus_maxima(dve, m, s_m, base):
    dve.tensor_reduce(m.mx1[:, :], m.mx[:, :].rearrange("p (u c) -> p u c", c=2), AX.X, ALU.max).then_inc(s_m, 1)
    dve.wait_ge(s_m, base + 1)
    dve.tensor_scalar(m.mparts[:, 0, :], m.mx1[:, :], -1.0, None, ALU.mult).then_inc(s_m, 1)
    dve.wait_ge(s_m, base + 2)
    dve.scalar_tensor_tensor(out=m.mrest[:, :], in0=m.mx1[:, :], scalar=-1.0, in1=m.mparts[:, 0, :],
                             op0=ALU.mult, op1=ALU.subtract).then_inc(s_m, 1)
    dve.wait_ge(s_m, base + 3)
    dve.tensor_copy(m.mparts[:, 1, :], m.mrest[:, :]).then_inc(s_m, 1)
    dve.wait_ge(s_m, base + 4)
    dve.tensor_tensor(m.mparts[:, 2, :], m.mrest[:, :], m.mparts[:, 1, :], ALU.subtract).then_inc(s_m, 1)


def store_maxima_rows(eng, m, par, signal):
    eng.dma_start(m.qst[par][NROW:NROW + MROW, :, :].rearrange("o h (t n) -> o (h t) n", n=P),
                  m.mT[0:MROW * NCH // 2, :]).then_inc(signal, 16)


def phase2(nc, m):
    with ExitStack() as ctx:
        def sem(name):
            return ctx.enter_context(nc.semaphore("p2_" + name))

        slots = [ctx.enter_context(nc.psum_tensor(f"p2_max{i}", [P, 2, 512], F32)) for i in range(2)]
        other = ctx.enter_context(nc.psum_tensor("p2_other", [P, 3, 512], F32))
        turned = ctx.enter_context(nc.psum_tensor("p2_turned", [P, P], BF16))
        ctxT, at = region(m.reg_f, 0, [P, DK, SP_])
        dft, at = region(m.reg_f, at, [P, 5 * DK, D])
        wT, at = region(m.reg_f, at, [P, 2 * DK, D])
        mid, at = region(m.reg_f, at, [P, 2 * DK, D])
        stage, _ = region(m.reg_a, 2 * ((G * SP_ + G * QW) // 2 + NS * P) + NS * H * 32, [P, 3, 512])

        s_load, s_dft, s_pads, s_mscore, s_mread, s_m, s_turn, s_mcopy, s_mrow = (
            sem(n) for n in ("load", "dft", "pads", "mscore", "mread", "m", "turn", "mcopy", "mrow"))
        s_unit, s_act, s_dve, s_vout, s_vload = (sem(n) for n in ("unit", "act", "dve", "vout", "vload"))
        s_stage = [sem(f"stage{i}") for i in range(3)]

        COS, SIN, COSD, SIND, NSIND = range(5)
        units = [("k", mt, c) for mt in range(DK) for c in range(4)]
        units += [("q", mt, c) for mt in range(DK) for c in range(4)]
        units += [("v", kt, 0) for kt in range(NS)]
        nstore = len(units)
        units += [("a", mt, 0) for mt in range(DK)] + [("b", mt, 0) for mt in range(DK)]
        units += [("f", mt, 0) for mt in range(DK)]
        nu = len(units)
        by_dve = [sum(x[0] == "v" for x in units[:u]) for u in range(nu + 1)]
        by_act = [u - by_dve[u] for u in range(nu + 1)]

        products = [(u, i, D if units[u][0] in "vabf" else 512)
                    for u in range(nu) for i in range(DK if units[u][0] in "kqv" else 2 * DK)]
        ahead = [x[:2] for x in products if x[0] < 3]
        products = [x for x in products if x[0] >= 3]
        share = 0.97 * sum(cost for _, _, cost in products) / NCH
        behind = [[] for _ in range(NCH + 1)]
        spent = 0
        for u, i, cost in products:
            behind[min(int(spent / share), NCH)].append((u, i))
            spent += cost

        def wait_read(eng, u):
            if units[u][0] == "v":
                eng.wait_ge(s_dve, by_dve[u + 1])
            else:
                eng.wait_ge(s_act, by_act[u + 1])

        block = ctx.enter_context(nc.Block())

        @block.sync
        def _(sp):
            load_q(sp, m, 0, 0, s_load)
            sp.dma_start(dft, m.dft).then_inc(s_dft, 16)
            sp.dma_start(wT, m.wf_T).then_inc(s_dft, 16)
            for u, (kind, a, c) in enumerate(units[:nstore]):
                wait_read(sp, u)
                w = min(512, S - c * 512)
                if kind == "k":
                    dst, src = m.ks_keep[:, a, c * 512:c * 512 + w], stage[:, u % 3, 0:w]
                elif kind == "q":
                    n = 4 if c < 3 else 1
                    dst = m.qs_keep.rearrange("(t p) (k n) -> p t k n", p=P, k=DK)[:, 4 * c:4 * c + n, a, :]
                    src = stage[:, u % 3, 0:n * P].rearrange("p (t n) -> p t n", t=n)
                else:
                    dst, src = m.vs_keep[:, a, :], stage[:, u % 3, 0:D]
                sp.dma_start(dst, src).then_inc(s_stage[u % 3], 16)
                if u < H // G:
                    dst = m.v_blocks[u * P:(u + 1) * P, :].rearrange("p (k h n) -> p k h n", k=NS, h=G)
                    sp.dma_start(dst, m.vaug[:, :, u * G:(u + 1) * G, :]).then_inc(s_vout, 16)
            sp.wait_ge(s_vout, 16 * (H // G))
            load_v(sp, m, 0, 0, s_vload)
            sp.wait_ge(s_mcopy, 1)
            store_maxima_rows(sp, m, 0, s_mrow)
            sp.wait_ge(s_mrow, 16)
            sp.wait_ge(s_vload, 16)
            for i in range(3):
                sp.wait_ge(s_stage[i], 16 * len(range(i, nstore, 3)))

        @block.gpsimd
        def _(pool):
            ones_rows(pool, m, 1, s_pads, 0)
            pool.wait_ge(s_pads, 2)

        @block.vector
        def _(dve):
            for n in range(NCH):
                dve.wait_ge(s_mscore, n + 1)
                dve.tensor_reduce(m.mx[:, n:n + 1], slots[n % 2][:, :, 0:CW], AX.XY, ALU.max).then_inc(s_mread, 1)
                for u, i in behind[n]:
                    if units[u][0] == "v" and i == DK - 1:
                        dve.wait_ge(s_unit, u + 1)
                        dve.wait_ge(s_stage[u % 3], 16 * (u // 3))
                        dve.tensor_tensor(stage[:, u % 3, 0:D], other[:, u % 3, 0:D], m.rows[:, RBVS, :],
                                          ALU.add).then_inc(s_dve, 1)
            dve.wait_ge(s_mread, NCH)
            minus_maxima(dve, m, s_m, 0)
            dve.wait_ge(s_turn, 1)
            dve.tensor_copy(m.mT[0:MROW * NCH // 2, :], turned[0:MROW * NCH // 2, :]).then_inc(s_mcopy, 1)

        @block.scalar
        def _(act):
            for u, (kind, a, c) in enumerate(units):
                if kind == "v":
                    continue
                act.wait_ge(s_unit, u + 1)
                if u < nstore and u >= 3:
                    act.wait_ge(s_stage[u % 3], 16 * (u // 3))
                if kind in "kq":
                    w = 512 if c < 3 else (STAIL if kind == "k" else P)
                    bias = m.cols[:, CBKS if kind == "k" else CBQS, a:a + 1]
                    ins = act.activation(stage[:, u % 3, 0:w], other[:, u % 3, 0:w], ACT.Identity, bias=bias)
                else:
                    out = m.filt[:, a, :] if kind == "f" else mid[:, (0 if kind == "a" else DK) + a, :]
                    ins = act.copy(out, other[:, u % 3, 0:D])
                ins.then_inc(s_act, 1)

        @block.tensor
        def _(pe):
            def product(u, i):
                kind, a, c = units[u]
                if u >= 3 and i == 0:
                    wait_read(pe, u - 3)
                out = other[:, u % 3, :]
                rows = slice(a * P, (a + 1) * P)
                if kind in "kq":
                    w = 512 if c < 3 else (STAIL if kind == "k" else P)
                    wn = KS if kind == "k" else QS
                    pairs = [(m.w1[:, wn * DK + k, rows], ctxT[:, k, c * 512:c * 512 + w]) for k in range(DK)]
                elif kind == "v":
                    w = D
                    pairs = [(ctxT[:, k, rows], m.w1[:, VS * DK + k, :]) for k in range(DK)]
                elif kind in "ab":
                    w = D
                    re, im = (COSD, NSIND) if kind == "a" else (SIND, COSD)
                    pairs = [(wT[:, k, rows], dft[:, re * DK + k, :]) for k in range(DK)]
                    pairs += [(wT[:, DK + k, rows], dft[:, im * DK + k, :]) for k in range(DK)]
                else:
                    w = D
                    pairs = [(dft[:, COS * DK + k, rows], mid[:, k, :]) for k in range(DK)]
                    pairs += [(dft[:, SIN * DK + k, rows], mid[:, DK + k, :]) for k in range(DK)]
                if kind == "a" and a == 0 and i == 0:
                    pe.wait_ge(s_dft, 32)
                if kind == "f" and a == 0 and i == 0:
                    pe.wait_ge(s_act, by_act[u])
                mm = pe.matmul(out[:, 0:w], *pairs[i], start=(i == 0), stop=(i == len(pairs) - 1))
                if i == len(pairs) - 1:
                    mm.then_inc(s_unit, 1)

            for u, i in ahead:
                product(u, i)
            pe.wait_ge(s_load, KQ_LOADS // 2)
            for n in range(NCH):
                if n >= 2:
                    pe.wait_ge(s_mread, n - 1)
                chunk_scores(pe, m, 0, 0, n, slots[n % 2], s_mscore)
                for u, i in behind[n]:
                    product(u, i)
            for u, i in behind[NCH]:
                product(u, i)
            pe.wait_ge(s_m, 5)
            pe.transpose(turned[0:MROW * NCH // 2, :], flat(m.mparts[:, :, :]), m.ident_b[:, :]).then_inc(s_turn, 1)


def phase3(nc, m):
    with ExitStack() as ctx:
        def sem(name):
            return ctx.enter_context(nc.semaphore("p3_" + name))

        sps = ctx.enter_context(nc.psum_tensor("p3_scores", [P, 2, 512], F32))
        ops = ctx.enter_context(nc.psum_tensor("p3_out", [P, 2, 512], F32))
        slots = [ctx.enter_context(nc.psum_tensor(f"p3_max{i}", [P, 2, 512], F32)) for i in range(2)]
        turned = slots[0][:, 0, 0:P // 2].bitcast(BF16)

        s_scores, s_exp, s_pv, s_oevac = (sem(n) for n in ("scores", "exp", "pv", "oevac"))
        s_mscore, s_mread, s_m, s_turn, s_mcopy, s_mrow, s_ostore = (
            sem(n) for n in ("mscore", "mread", "m", "turn", "mcopy", "mrow", "ostore"))
        s_kqdone, s_ofree, s_last = (sem(n) for n in ("kqdone", "ofree", "last"))
        s_qload, s_kload, s_vload = ([sem(f"{n}{i}") for i in range(2)] for n in ("qload", "kload", "vload"))

        UNITS = 2 * G
        PER = NS * UNITS
        PVS = 2 * NS
        PVC = 4
        J_TURN = 4
        U_MAX = ((8, 94), (12, 94))

        def max_chunks(par, u):
            lo, hi = U_MAX[par]
            return [n for n in range(NCH) if lo + n * (hi - lo) // (NCH - 1) == u]

        def blocks(eng, body):
            with eng.Fori(0, NB // 2 - 1) as i:
                body(i * 2, 0, i, True)
                body(i * 2 + 1, 1, i, True)
            body(NB - 2, 0, NB // 2 - 1, True)
            body(NB - 1, 1, NB // 2 - 1, False)

        def store_result(eng, i, par, signal):
            for h in range(G):
                dst = m.o_all[:, bass.ds(par * D + i * (G * HD) + h * HD, HD), :]
                eng.dma_start(dst, flat(m.oT[32 * h:32 * (h + 1), :, :])).then_inc(signal, 16)

        block = ctx.enter_context(nc.Block())

        @block.sync
        def _(sp):
            sp.sem_inc(s_mrow, 16)
            sp.sem_inc(s_vload[0], 16)

            def body(b, par, i, more):
                if more:
                    sp.wait_ge(s_kqdone, b + 1)
                    loads = ((load_q, s_qload), (load_k, s_kload))
                    for load, signal in loads if par == 0 else loads[::-1]:
                        load(sp, m, i + par, 1 - par, signal[1 - par])
                    sp.wait_ge(s_pv, b * PVS + PVC)
                    load_v(sp, m, i + par, 1 - par, s_vload[1 - par])
                    if isinstance(b, int):
                        for e in range(2):
                            sp.dma_start(expert_weights(m, e), m.w_exp[e * P:(e + 1) * P, :]).then_inc(s_last, 16)
                    sp.wait_ge(s_mcopy, b + 2)
                    store_maxima_rows(sp, m, 1 - par, s_mrow)

            blocks(sp, body)
            sp.wait_ge(s_oevac, 2 * NB + 2)
            store_result(sp, NB // 2 - 1, 1, s_last)
            sp.wait_ge(s_last, 16 * (G + 2))

        @block.gpsimd
        def _(pool):
            def body(b, par, i, more):
                if not more:
                    return
                wait_apart(pool, s_oevac, 2 * b + 4, m.passed)
                store_result(pool, i, par, s_ostore)
                pool.wait_ge(s_ostore, (b + 1) * (16 * G))
                pool.sem_inc(s_ofree, 1)

            blocks(pool, body)

        @block.vector
        def _(dve):
            dve.sem_inc(s_mread, 2)
            dve.sem_inc(s_mcopy, 1)
            dve.sem_inc(s_oevac, 2)
            dve.sem_inc(s_ofree, 1)

            def body(b, par, i, more):
                if more:
                    maxima(b)
                dve.wait_ge(s_ofree, b + 1)
                for qb in range(2):
                    dve.wait_ge(s_pv, b * PVS + PVS + PVC - 1 + qb)
                    dve.tensor_copy(m.oT[:, qb, :], ops[:, qb, :]).then_inc(s_oevac, 1)

            def maxima(b):
                for n in range(NCH):
                    dve.wait_ge(s_mscore, b * NCH + n + 1)
                    dve.tensor_reduce(m.mx[:, n:n + 1], slots[n % 2][:, :, 0:CW], AX.XY, ALU.max).then_inc(s_mread, 1)
                dve.wait_ge(s_mread, b * NCH + NCH + 2)
                minus_maxima(dve, m, s_m, b * 5)
                dve.wait_ge(s_turn, b + 1)
                dve.wait_ge(s_mrow, (b + 1) * 16)
                dve.tensor_copy(m.mT[0:MROW * NCH // 2, :], turned[0:MROW * NCH // 2, :]).then_inc(s_mcopy, 1)

            blocks(dve, body)

        @block.scalar
        def _(act):

            def exps(b, par, kt):
                buf = m.prob[(par * NS + kt) % 2]
                for j in range(UNITS):
                    h, qb = j // 2, j % 2
                    u = kt * UNITS + j
                    if h == 0:
                        act.wait_ge(s_pv, b * PVS + 2 * kt + qb + 1)
                    act.wait_ge(s_scores, b * PER + u + 1)
                    act.activation(buf[:, h, qb * 512:(qb + 1) * 512], sps[:, u % 2, :], ACT.Exp).then_inc(s_exp, 1)

            def body(b, par, i, more):
                for kt in range(1, NS):
                    exps(b, par, kt)
                if more:
                    exps(b + 1, 1 - par, 0)
            warm_up(act, m, ACT.Exp)
            exps(0, 0, 0)
            blocks(act, body)

        @block.tensor
        def _(pe):
            pe.sem_inc(s_pv, PVC)
            pe.sem_inc(s_kqdone, 1)

            def pv(b, par, i, kt, quarter):
                qb, first = quarter // 2, quarter % 2 == 0
                if first:
                    pe.wait_ge(s_exp, b * PER + kt * UNITS + 2 * (G - 1) + qb + 1)
                if kt == 0 and quarter == 0:
                    pe.wait_ge(s_vload[par], i * 16 + 16)
                if kt == 0 and first:
                    pe.wait_ge(s_oevac, b * 2 + qb + 1)
                buf = m.prob[(par * NS + kt) % 2]
                half = slice(quarter % 2 * 256, quarter % 2 * 256 + 256)
                for h in range(G):
                    mm = pe.matmul(ops[32 * h:32 * h + 32, qb, half], m.vb[par][:, kt, 32 * h:32 * h + 32],
                                   buf[:, h, quarter * 256:quarter * 256 + 256],
                                   start=(kt == 0 and first), stop=(kt == NS - 1), skip_group_check=True)
                    if kt == NS - 1 and quarter == 0 and h == 0:
                        mm.then_inc(s_kqdone, 1)
                if not first:
                    mm.then_inc(s_pv, 1)

            def scores(b, par, kt, j):
                h, qb = j // 2, j % 2
                u = kt * UNITS + j
                if not (isinstance(b, int) and b * PER + u < 2):
                    pe.wait_ge(s_exp, b * PER + u - 1)
                pe.matmul(sps[:, u % 2, :], m.kst[par][0:NROW + MROW, h, kt * P:(kt + 1) * P],
                          m.qst[par][0:NROW + MROW, h, qb * 512:(qb + 1) * 512],
                          start=True, stop=True).then_inc(s_scores, 1)

            def body(b, par, i, more):
                for kt in range(1, NS):
                    for j in range(UNITS):
                        scores(b, par, kt, j)
                        for n in max_chunks(par, kt * UNITS + j) if more else []:
                            if n == 0:
                                pe.wait_ge(s_mcopy, b + 1)
                                wait_loaded(pe, i, s_qload[1 - par])
                                if par == 1:
                                    wait_loaded(pe, i, s_kload[0])
                            pe.wait_ge(s_mread, b * NCH + n + 1)
                            chunk_scores(pe, m, 1 - par, 0, n, slots[n % 2], s_mscore)
                        if j % 2 == 1:
                            pv(b, par, i, kt - 1, j // 2)
                        if more and kt == NS - 1 and j == J_TURN:
                            pe.wait_ge(s_m, b * 5 + 5)
                            pe.transpose(turned[0:MROW * NCH // 2, :], flat(m.mparts[:, :, :]),
                                         m.ident_b[:, :]).then_inc(s_turn, 1)
                for quarter in range(4):
                    pv(b, par, i, NS - 1, quarter)
                    if more and quarter == 1:
                        if par == 0:
                            wait_loaded(pe, i, s_kload[1])
                        pe.wait_ge(s_mrow, (b + 2) * 16)
                    if more and quarter >= 1:
                        scores(b + 1, 1 - par, 0, 2 * quarter - 2)
                        scores(b + 1, 1 - par, 0, 2 * quarter - 1)
                if more:
                    for j in range(6, UNITS):
                        scores(b + 1, 1 - par, 0, j)

            def wait_loaded(pe, i, signal):
                pe.wait_ge(signal, i * (KQ_LOADS // 2) + KQ_LOADS // 2)

            for j in range(UNITS):
                scores(0, 0, 0, j)
            blocks(pe, body)


def expert_weights(m, par):
    n = 2 * DK * F + NF * D
    return m.reg_f[:, par * n:(par + 1) * n]


def phase4(nc, m):
    with ExitStack() as ctx:
        def sem(name):
            return ctx.enter_context(nc.semaphore("p4_" + name))

        def ps(name):
            return ctx.enter_context(nc.psum_tensor("p4_" + name, [P, 2, 512], F32))

        def small(name, shape):
            return ctx.enter_context(nc.sbuf_tensor("p4_" + name, shape, F32))

        aps, tps, gps, dps = ps("attn"), ps("turn"), ps("gate_up"), ps("down")
        w = [expert_weights(m, i) for i in range(2)]
        w13 = [x[:, 0:2 * DK * F].rearrange("p (a f) -> p a f", f=F) for x in w]
        w2 = [x[:, 2 * DK * F:].rearrange("p (a d) -> p a d", d=D) for x in w]
        at = 0
        oT, at = region(m.reg_a, at, [P, 2, DK, EW])
        den, at = region(m.reg_a, at, [P, 2, DK, EW])
        rec, at = region(m.reg_a, at, [P, DK, EW])
        on, at = region(m.reg_a, at, [P, 2, DK, EW])
        tmp, at = region(m.reg_a, at, [P, 2, D])
        xn2, at = region(m.reg_a, at, [P, 2, D])
        xn3, at = region(m.reg_a, at, [P, 2, D])
        xn2T, at = region(m.reg_a, at, [P, 2, DK, EW])
        sg, at = region(m.reg_a, at, [P, 2, EW])
        hT, at = region(m.reg_a, at, [P, NF, EW])
        st = [small(f"stats{i}", [P, 2, 6]) for i in range(2)]
        mv = [small(f"mv{i}", [P, 2, 2]) for i in range(2)]
        var = [small(f"var{i}", [P, 2]) for i in range(2)]
        rstd = [small(f"rstd{i}", [P, 2]) for i in range(2)]

        s_w = [sem(f"w{i}") for i in range(2)]
        s_o = [sem(f"o{i}") for i in range(2)]
        s_rec, s_onorm, s_attn, s_bo, s_x1 = (sem(n) for n in ("rec", "onorm", "attn", "bo", "x1"))
        s_turn, s_copy, s_gu, s_silu, s_h, s_down, s_x2 = (
            sem(n) for n in ("turn", "copy", "gu", "silu", "h", "down", "x2"))
        s_st, s_ag, s_var, s_rstd, s_norm = ([sem(f"{n}{i}") for i in range(2)] for n in ("st", "ag", "var", "rstd", "norm"))

        def experts(eng, body):
            body(0, 0, 0, True, False)
            with eng.Fori(0, E // 2 - 1) as i:
                body(i * 2 + 1, 1, i, False, False)
                body(i * 2 + 2, 0, i + 1, False, False)
            body(E - 1, 1, E // 2 - 1, False, True)

        def load_weights(eng, e, par):
            eng.dma_start(w[par], m.w_exp[bass.ds(e * P, P), :]).then_inc(s_w[par], 16)

        def load_attn(eng, par, half):
            for a, dst in enumerate((oT, den)):
                rows = m.o_all[a, par * D:(par + 1) * D, :].rearrange("(k p) n -> p k n", p=P)
                eng.dma_start(dst[:, par, :, :], rows[:, :, bass.ds(half * EW, EW)]).then_inc(s_o[par], 16)

        block = ctx.enter_context(nc.Block())

        @block.sync
        def _(sp):
            load_attn(sp, 0, 0)
            for i in range(2):
                sp.sem_inc(s_w[i], 16)

            def body(e, par, half, first, last):
                if last:
                    return
                if not first:
                    sp.wait_ge(s_onorm, e)
                load_attn(sp, 1 - par, half + par)
                if not first:
                    sp.wait_ge(s_down, e * 2)
                    load_weights(sp, e + 1, 1 - par)

            experts(sp, body)

        @block.gpsimd
        def _(pool):
            def scale(i, n):
                pool.wait_ge(s_var[i], n + 1)
                pool.tensor_tensor(rstd[i][:, :], var[i][:, :], m.neghalf[:, 0:2], ALU.pow).then_inc(s_rstd[i], 1)

            scale(0, 0)

            def body(e, par, half, first, last):
                if not first:
                    scale(1, e - 1)
                if not last:
                    scale(0, e + 1)

            experts(pool, body)
            scale(1, E - 1)

        @block.vector
        def _(dve):
            dve.sem_inc(s_h, 2)
            dve.sem_inc(s_x2, 2)

            def xs(e, t):
                return m.x[:, bass.ds(e * 2 + t, 1), :].rearrange("p o d -> p (o d)")

            def moments(i, e, s_src):
                for t in range(2):
                    wait_apart(dve, s_src, e * 2 + t + (1 if i == 0 else 3), m.passed)
                    dve.bn_stats(st[i][:, t, :], xs(e, t)).then_inc(s_st[i], 1)
                for t in range(2):
                    wait_apart(dve, s_st[i], e * 2 + t + 1, m.passed)
                    dve.bn_aggr(mv[i][:, t, :], st[i][:, t, :]).then_inc(s_ag[i], 1)
                dve.wait_ge(s_ag[i], e * 2 + 2)
                dve.tensor_scalar(var[i][:, :], mv[i][:, :, 1], EPS, None, ALU.add).then_inc(s_var[i], 1)

            def norm(i, e, out):
                dve.wait_ge(s_rstd[i], e + 1)
                for t in range(2):
                    dve.tensor_scalar(out[:, t, :], xs(e, t), mv[i][:, t, 0:1], rstd[i][:, t:t + 1],
                                      ALU.subtract, ALU.mult).then_inc(s_norm[i], 1)

            def attn_result(e, par, half):
                dve.wait_ge(s_o[par], half * 32 + 32)
                dve.reciprocal(rec, den[:, par, :, :]).then_inc(s_rec, 1)
                dve.wait_ge(s_rec, e + 1)
                dve.tensor_tensor(on[:, par, :, :], oT[:, par, :, :], rec, ALU.mult).then_inc(s_onorm, 1)

            def residual1(e):
                for t in range(2):
                    dve.wait_ge(s_attn, e * 2 + t + 1)
                    dve.tensor_tensor(tmp[:, t, :], aps[:, t, 0:D], m.rows[:, RBO, :], ALU.add).then_inc(s_bo, 1)
                for t in range(2):
                    dve.wait_ge(s_bo, e * 2 + t + 1)
                    dve.scalar_tensor_tensor(out=xs(e, t), in0=tmp[:, t, :], scalar=m.gains[:, 0:1], in1=xs(e, t),
                                             op0=ALU.mult, op1=ALU.add).then_inc(s_x1, 1)

            def hidden(e, f):
                r = P if f < NF - 1 else FTAIL
                dve.wait_ge(s_silu, e * NF + f + 1)
                dve.tensor_tensor(hT[0:r, f, :], sg[0:r, f % 2, :], gps[0:r, f % 2, EW:2 * EW], ALU.mult).then_inc(s_h, 1)

            attn_result(0, 0, 0)
            residual1(0)
            moments(0, 0, s_x1)
            norm(0, 0, xn2)

            def residual2(e):
                for t in range(2):
                    dve.wait_ge(s_down, e * 2 + t + 1)
                    dve.scalar_tensor_tensor(out=xs(e, t), in0=dps[:, t, 0:D], scalar=m.gains[:, 2:3], in1=xs(e, t),
                                             op0=ALU.mult, op1=ALU.add).then_inc(s_x2, 1)

            def body(e, par, half, first, last):
                if not last:
                    if not first:
                        dve.wait_ge(s_attn, e * 2)
                    attn_result(e + 1, 1 - par, half + par)
                if not first:
                    residual2(e - 1)
                    moments(1, e - 1, s_x2)
                hidden(e, 0)
                if not first:
                    norm(1, e - 1, xn3)
                hidden(e, 1)
                if not last:
                    residual1(e + 1)
                hidden(e, 2)
                if not last:
                    moments(0, e + 1, s_x1)
                    dve.wait_ge(s_copy, e * 4 if not first else 2)
                    norm(0, e + 1, xn2)
                for f in range(3, NF):
                    hidden(e, f)

            experts(dve, body)
            residual2(E - 1)
            moments(1, E - 1, s_x2)
            norm(1, E - 1, xn3)

        @block.scalar
        def _(act):
            def copies(q, outs):
                for t in range(2):
                    act.wait_ge(s_turn, q + t + 1)
                    act.copy(outs[t], tps[:, t, 0:D].rearrange("p (k n) -> p k n", k=DK)).then_inc(s_copy, 1)

            def into_xn2T(par):
                return [xn2T[:, par, :, t * P:(t + 1) * P] for t in range(2)]

            def into_xnT(e):
                return [m.xnT[:, :, bass.ds(e * EW + t * P, P)] for t in range(2)]

            def silu(e, f):
                r = P if f < NF - 1 else FTAIL
                act.wait_ge(s_gu, e * NF + f + 1)
                act.wait_ge(s_h, e * NF + f + 1)
                act.activation(sg[0:r, f % 2, :], gps[0:r, f % 2, 0:EW], ACT.Silu).then_inc(s_silu, 1)

            warm_up(act, m, ACT.Silu)
            copies(0, into_xn2T(0))

            def body(e, par, half, first, last):
                for f in range(3):
                    silu(e, f)
                if not first:
                    copies(e * 4, into_xnT(e - 1))
                for f in range(3, NF - 1):
                    silu(e, f)
                if not last:
                    copies(e * 4 + 2, into_xn2T(1 - par))
                silu(e, NF - 1)
                if last:
                    copies(e * 4 + 2, into_xnT(e))

            experts(act, body)

        @block.tensor
        def _(pe):
            def turn(q, i, n, src):
                for t in range(2):
                    pe.wait_ge(s_norm[i], n + t + 1)
                    pe.wait_ge(s_copy, q + t - 1 if not isinstance(q, int) or q >= 2 else 0)
                    for k in range(DK):
                        mm = pe.transpose(tps[:, t, k * P:(k + 1) * P], src[:, t, k * P:(k + 1) * P], m.ident[:, :])
                    mm.then_inc(s_turn, 1)

            def attn_out(e, par, first):
                pe.wait_ge(s_onorm, e + 1)
                for t in range(2):
                    if not first:
                        pe.wait_ge(s_bo, e * 2 + t - 1)
                    for k in range(DK):
                        mm = pe.matmul(aps[:, t, 0:D], on[:, par, k, t * P:(t + 1) * P], m.w0[:, WO * DK + k, :],
                                       start=(k == 0), stop=(k == DK - 1))
                    mm.then_inc(s_attn, 1)

            def gate_up(e, par, f):
                r = P if f < NF - 1 else FTAIL
                pe.wait_ge(s_h, e * NF + f + 1)
                for g in range(2):
                    for k in range(DK):
                        mm = pe.matmul(gps[0:r, f % 2, g * EW:(g + 1) * EW], w13[par][:, g * DK + k, f * P:f * P + r],
                                       xn2T[:, par, k, :], start=(k == 0), stop=(k == DK - 1))
                mm.then_inc(s_gu, 1)

            attn_out(0, 0, True)
            turn(0, 0, 0, xn2)

            def body(e, par, half, first, last):
                pe.wait_ge(s_w[par], half * 16 + 16)
                pe.wait_ge(s_copy, e * 4 if not first else 2)
                for f in range(2):
                    gate_up(e, par, f)
                if not last:
                    attn_out(e + 1, 1 - par, False)
                gate_up(e, par, 2)
                if not first:
                    turn(e * 4, 1, e * 2 - 2, xn3)
                for f in range(3, NF - 1):
                    gate_up(e, par, f)
                if not last:
                    turn(e * 4 + 2, 0, e * 2 + 2, xn2)
                gate_up(e, par, NF - 1)
                pe.wait_ge(s_h, e * NF + NF + 1)
                for t in range(2):
                    pe.wait_ge(s_x2, e * 2 + t + 1)
                    for f in range(NF):
                        if t == 0 and f == NF - 1:
                            pe.wait_ge(s_h, e * NF + NF + 2)
                        r = P if f < NF - 1 else FTAIL
                        mm = pe.matmul(dps[:, t, 0:D], hT[0:r, f, t * P:(t + 1) * P], w2[par][0:r, f, :],
                                       start=(f == 0), stop=(f == NF - 1))
                    mm.then_inc(s_down, 1)
                if last:
                    turn(e * 4 + 2, 1, e * 2, xn3)

            experts(pe, body)


def phase5(nc, m):
    at = 0
    m.ks, at = region(m.reg_a, at, [P, DK, S])
    m.vs, at = region(m.reg_a, at, [P, NS, D])
    m.ctx_q, at = region(m.reg_a, at, [P, 2, DK, P])
    m.free_a = at
    m.kc, at = region(m.reg_f, 0, [P, DK, T])
    m.vc, at = region(m.reg_f, at, [P, NT, D])
    with ExitStack() as ctx:
        def sem(name):
            return ctx.enter_context(nc.semaphore("p5_" + name))

        kps = ctx.enter_context(nc.psum_tensor("p5_k", [P, 2, 512], F32))
        vps = ctx.enter_context(nc.psum_tensor("p5_v", [P, 2, 512], F32))
        s_back, s_k, s_kread, s_v, s_vread = (sem(n) for n in ("back", "k", "kread", "v", "vread"))
        block = ctx.enter_context(nc.Block())

        @block.sync
        def _(sp):
            sp.dma_start(m.ks, m.ks_keep).then_inc(s_back, 16)
            sp.dma_start(m.vs, m.vs_keep).then_inc(s_back, 16)
            sp.wait_ge(s_back, 32)

        @block.scalar
        def _(act):
            for n in range(8):
                mt, tb = n % 2, n // 2
                act.wait_ge(s_k, n + 1)
                act.activation(m.kc[:, mt, tb * 512:(tb + 1) * 512], kps[:, n % 2, :], ACT.Identity,
                               bias=m.cols[:, CBKC, mt:mt + 1]).then_inc(s_kread, 1)

        @block.vector
        def _(dve):
            for t in range(NT):
                dve.wait_ge(s_v, t + 1)
                dve.tensor_tensor(m.vc[:, t, :], vps[:, t % 2, 0:D], m.rows[:, RBVC, :], ALU.add).then_inc(s_vread, 1)

        @block.tensor
        def _(pe):
            for n in range(8):
                mt, tb = n % 2, n // 2
                if n >= 2:
                    pe.wait_ge(s_kread, n - 1)
                for k in range(DK):
                    mm = pe.matmul(kps[:, n % 2, :], m.w1[:, KC * DK + k, mt * P:(mt + 1) * P],
                                   m.xnT[:, k, tb * 512:(tb + 1) * 512], start=(k == 0), stop=(k == DK - 1))
                mm.then_inc(s_k, 1)
                for t in (2 * n, 2 * n + 1):
                    if t >= 2:
                        pe.wait_ge(s_vread, t - 1)
                    for k in range(DK):
                        mm = pe.matmul(vps[:, t % 2, 0:D], m.xnT[:, k, t * P:(t + 1) * P], m.w1[:, VC * DK + k, :],
                                       start=(k == 0), stop=(k == DK - 1))
                    mm.then_inc(s_v, 1)


def attention1(nc, m, side, ntile, nkey, nkt):
    tok = side == "tok"
    kT, v, keep = (m.ks, m.vs, m.c2s) if tok else (m.kc, m.vc, m.s2c)
    with ExitStack() as ctx:
        def sem(name):
            return ctx.enter_context(nc.semaphore(f"{side}_{name}"))

        def ps(name, n):
            return ctx.enter_context(nc.psum_tensor(f"{side}_{name}", [P, n, 512], F32))

        def small(name, shape):
            return ctx.enter_context(nc.sbuf_tensor(f"{side}_{name}", shape, F32))

        sps, tps, ops, qps = ps("scores", 4), ps("turn", 2), ps("out", 1), ps("q", 1)
        at = m.free_a
        prob, at = region(m.reg_a, at, [P, 2, NT * P])
        pT, at = region(m.reg_a, at, [P, NT, P])
        if tok:
            qb, at = region(m.reg_a, at, [P, 2, DK, P])
        else:
            qb = m.ctx_q
        ob, at = region(m.reg_a, at, [P, 2, D])
        mx, nm, total, rec = (small(n, [P, 2]) for n in ("mx", "nm", "total", "rec"))

        s_scores, s_mx, s_nm, s_exp, s_turn, s_pv, s_rec, s_o = (
            sem(n) for n in ("scores", "mx", "nm", "exp", "turn", "pv", "rec", "o"))
        s_pc = [sem(f"pc{i}") for i in range(2)]
        if tok:
            s_q, s_qproj, s_next = sem("q"), sem("qproj"), sem("next")
        else:
            s_qload = [sem(f"qload{i}") for i in range(2)]
        s_store = [sem(f"store{i}") for i in range(2)]
        groups = [range(4 * j, min(4 * j + 4, nkt)) for j in range(4)]
        chunks = [(c * 512, min(512, nkey - c * 512)) for c in range(4)]

        def width(kt):
            return min(P, nkey - kt * P)

        def tiles(eng, body):
            body(0, 0, 0, True, False)
            with eng.Fori(0, (ntile - 1) // 2) as i:
                body(i * 2 + 1, 1, i, False, False)
                body(i * 2 + 2, 0, i + 1, False, ntile % 2 == 1 and None)
            if ntile % 2 == 0:
                body(ntile - 1, 1, ntile // 2 - 1, False, True)

        LAST = ntile - 1
        LPAR = LAST % 2

        block = ctx.enter_context(nc.Block())

        @block.sync
        def _(sp):
            def load(t, par, signal):
                sp.dma_start(m.ctx_q[:, par, :, :], m.qs_keep[bass.ds(t * P, P), :].rearrange("p (k n) -> p k n", k=DK)
                             ).then_inc(signal, 16)

            def store(t, par):
                sp.wait_ge(s_o, t + 2)
                sp.dma_start(keep[bass.ds(t * P, P), :], ob[:, par, :]).then_inc(s_store[par], 16)

            def step(t, par, more):
                if not tok and more:
                    sp.wait_ge(s_scores, t + 2)
                    load(t + 2, par, s_qload[par])
                store(t, par)

            for i in range(2):
                sp.sem_inc(s_store[i], 16)
                if tok:
                    load(i, i, s_next)
                else:
                    sp.sem_inc(s_qload[i], 16)
            with sp.Fori(0, (ntile - 2) // 2) as i:
                step(i * 2, 0, True)
                step(i * 2 + 1, 1, True)
            for t in range(2 * ((ntile - 2) // 2), ntile):
                step(t, t % 2, t + 2 < ntile)
            sp.wait_ge(s_store[0], 16 * (-(-ntile // 2) + 1))
            sp.wait_ge(s_store[1], 16 * (ntile // 2 + 1))
            if tok:
                sp.wait_ge(s_next, 32)

        @block.vector
        def _(dve):
            def copy_group(t, j):
                w = sum(width(kt) for kt in groups[j])
                n = len(groups[j])
                dve.wait_ge(s_turn, t * 4 + j + 1)
                if w == n * P:
                    src, dst = tps[:, j % 2, 0:w], flat(pT[:, 4 * j:4 * j + n, :])
                else:
                    src, dst = tps[0:w, j % 2, 0:P], pT[0:w, 4 * j, :]
                dve.tensor_copy(dst, src).then_inc(s_pc[0], 1)

            def maximum(t, par):
                dve.wait_ge(s_scores, t + 2)
                dve.tensor_reduce(mx[:, par:par + 1], flat(sps[:, :, :])[:, 0:nkey], AX.X, ALU.max).then_inc(s_mx, 1)
                dve.wait_ge(s_mx, t + 1)
                dve.tensor_scalar(nm[:, par:par + 1], mx[:, par:par + 1], -SC1, None, ALU.mult).then_inc(s_nm, 1)

            def finish(t, par, half):
                dve.wait_ge(s_exp, t + 1)
                dve.reciprocal(rec[:, par:par + 1], total[:, par:par + 1]).then_inc(s_rec, 1)
                dve.wait_ge(s_rec, t + 1)
                dve.wait_ge(s_pv, t + 1)
                dve.wait_ge(s_store[par], half * 16 + 16)
                dve.tensor_scalar(ob[:, par, :], ops[:, 0, 0:D], rec[:, par:par + 1], None, ALU.mult).then_inc(s_o, 1)

            def body(t, par, half, first, last):
                if not first:
                    copy_group(t - 1, 0)
                maximum(t, par)
                if not first:
                    copy_group(t - 1, 2)
                    finish(t - 1, 1 - par, half + par - 1 if par == 0 else half)

            dve.sem_inc(s_pc[0], 1)
            dve.sem_inc(s_o, 1)
            tiles(dve, body)
            copy_group(LAST, 0)
            copy_group(LAST, 2)
            finish(LAST, LPAR, LAST // 2)

        @block.scalar
        def _(act):
            def q_keep(t, par):
                act.wait_ge(s_qproj, t + 1)
                for mt in range(DK):
                    ins = act.activation(qb[:, par, mt, :], qps[:, 0, mt * P:(mt + 1) * P], ACT.Identity,
                                         bias=m.cols[:, CBQC, mt:mt + 1])
                ins.then_inc(s_q, 1)

            def copy_group(t, j):
                act.wait_ge(s_turn, t * 4 + j + 1)
                n = len(groups[j])
                w = width(groups[j][-1])
                if w == P:
                    src, dst = tps[:, j % 2, 0:n * P], flat(pT[:, 4 * j:4 * j + n, :])
                else:
                    src, dst = tps[0:w, j % 2, 0:P], pT[0:w, 4 * j, :]
                act.copy(dst, src).then_inc(s_pc[1], 1)

            def exps(t, par):
                act.wait_ge(s_nm, t + 1)
                act.activation(prob[:, par, 0:nkey], flat(sps[:, :, :])[:, 0:nkey], ACT.Exp, bias=nm[:, par:par + 1],
                               scale=SC1, accum_out=total[:, par:par + 1]).then_inc(s_exp, 1)

            warm_up(act, m, ACT.Exp)
            if tok:
                q_keep(0, 0)

            def body(t, par, half, first, last):
                if tok and last is not True:
                    q_keep(t + 1, 1 - par)
                if not first:
                    copy_group(t - 1, 1)
                exps(t, par)
                if not first:
                    copy_group(t - 1, 3)

            act.sem_inc(s_pc[1], 1)
            tiles(act, body)
            copy_group(LAST, 1)
            copy_group(LAST, 3)

        @block.tensor
        def _(pe):
            def q_proj(t):
                pe.wait_ge(s_q, t)
                for mt in range(DK):
                    for k in range(DK):
                        mm = pe.matmul(qps[:, 0, mt * P:(mt + 1) * P], m.w1[:, QC * DK + k, mt * P:(mt + 1) * P],
                                       m.xnT[:, k, bass.ds(t * P, P)], start=(k == 0), stop=(k == DK - 1))
                mm.then_inc(s_qproj, 1)

            def scores(t, par, half, first):
                if tok:
                    pe.wait_ge(s_q, t + 1)
                else:
                    pe.wait_ge(s_qload[par], half * 16 + 16)
                if not first:
                    pe.wait_ge(s_exp, t)
                for c, (o, w) in enumerate(chunks):
                    if c == 3 and not first:
                        turn_group(t - 1, 1 - par, 0)
                    for k in range(DK):
                        mm = pe.matmul(sps[:, c, 0:w], qb[:, par, k, :], kT[:, k, o:o + w],
                                       start=(k == 0), stop=(k == DK - 1))
                mm.then_inc(s_scores, 1)

            def turn_group(t, par, j):
                pe.wait_ge(s_pc[j % 2], t * 2 + j // 2 + 1)
                for i, kt in enumerate(groups[j]):
                    w = width(kt)
                    mm = pe.transpose(tps[0:w, j % 2, i * P:(i + 1) * P], prob[:, par, kt * P:kt * P + w], m.ident[:, :])
                mm.then_inc(s_turn, 1)

            def pv_group(t, j):
                pe.wait_ge(s_pc[j % 2], t * 2 + j // 2 + 2)
                for kt in groups[j]:
                    w = width(kt)
                    mm = pe.matmul(ops[:, 0, 0:D], pT[0:w, kt, :], v[0:w, kt, :], start=(kt == 0), stop=(kt == nkt - 1))
                return mm

            def values(t, par):
                turn_group(t, par, 1)
                pe.wait_ge(s_o, t + 1)
                pv_group(t, 0)
                turn_group(t, par, 2)
                pv_group(t, 1)
                turn_group(t, par, 3)
                pv_group(t, 2)
                pv_group(t, 3).then_inc(s_pv, 1)

            pe.sem_inc(s_scores, 1)
            if tok:
                q_proj(0)

            def body(t, par, half, first, last):
                scores(t, par, half, first)
                if tok and last is not True:
                    q_proj(t + 1)
                if not first:
                    values(t - 1, 1 - par)

            tiles(pe, body)
            pe.wait_ge(s_exp, LAST + 1)
            turn_group(LAST, LPAR, 0)
            values(LAST, LPAR)


def phase8(nc, m):
    with ExitStack() as ctx:
        def sem(name):
            return ctx.enter_context(nc.semaphore("p8_" + name))

        def ps(name):
            return ctx.enter_context(nc.psum_tensor("p8_" + name, [P, 512], F32))

        def small(name, shape):
            return ctx.enter_context(nc.sbuf_tensor("p8_" + name, shape, F32))

        ips, cps, eps_, gps, xps, yps = (ps(n) for n in ("stretch", "turn_c", "stretch_T", "gate", "turn_x", "filter"))
        at = 0
        stretch, at = region(m.reg_f, at, [P, 2, P])
        win, at = region(m.reg_f, at, [P, 2, D])
        cb, at = region(m.reg_f, at, [P, 2, D])
        sbuf, at = region(m.reg_f, at, [P, 2, D])
        gT, at = region(m.reg_f, at, [P, 2, 2 * DK, P])
        dif, at = region(m.reg_f, at, [P, 2, D])
        gate, at = region(m.reg_f, at, [P, D])
        mul, at = region(m.reg_f, at, [P, D])
        base, at = region(m.reg_f, at, [P, 2, D])
        scaled, at = region(m.reg_f, at, [P, D])
        ones, at = region(m.reg_f, at, [P, P])
        fbias, at = region(m.reg_f, at, [P, D])
        xb, at = region(m.reg_f, at, [P, 2, D])
        xn, at = region(m.reg_f, at, [P, D])
        xT, at = region(m.reg_f, at, [P, DK, P])
        ob, at = region(m.reg_f, at, [P, 2, D])
        st, mv, var, rstd = small("st", [P, 6]), small("mv", [P, 2]), small("var", [P, 1]), small("rstd", [P, 1])

        s_in = [sem(f"in{i}") for i in range(2)]
        s_cin = [sem(f"cin{i}") for i in range(2)]
        s_store = [sem(f"store{i}") for i in range(2)]
        s_stretch, s_scopy, s_tc, s_tccopy, s_ts, s_tscopy, s_gate, s_sig, s_const = (
            sem(n) for n in ("stretch", "scopy", "tc", "tccopy", "ts", "tscopy", "gate", "sig", "const"))
        s_scaled, s_base, s_xb = (sem(n) for n in ("scaled", "base", "xb"))
        s_dif, s_mul, s_x3, s_st, s_mv, s_var, s_rstd, s_norm = (
            sem(n) for n in ("dif", "mul", "x3", "st", "mv", "var", "rstd", "norm"))
        s_tx, s_txcopy, s_y, s_out = (sem(n) for n in ("tx", "txcopy", "y", "out"))

        def tiles(eng, body):
            body(0, 0, 0, (True, False, False))
            body(1, 1, 0, (True, True, False))
            with eng.Fori(0, NT // 2 - 1) as i:
                body(i * 2 + 2, 0, i + 1, (True, True, True))
                body(i * 2 + 3, 1, i + 1, (True, True, True))
            body(NT, 0, NT // 2, (False, True, True))
            body(NT + 1, 1, NT // 2, (False, False, True))

        def xs(t):
            return m.x[:, bass.ds(t, 1), :].rearrange("p o d -> p (o d)")

        block = ctx.enter_context(nc.Block())

        @block.sync
        def _(sp):
            def load(t, par):
                sp.dma_start(stretch[:, par, :], m.interp[bass.ds(t * P, P), :]).then_inc(s_in[par], 16)
                sp.dma_start(win[:, par, :], m.s2c[bass.ds(t * STRIDE, P), :]).then_inc(s_in[par], 16)

            def load_c(t, par):
                sp.dma_start(cb[:, par, :], m.c2s[bass.ds(t * P, P), :]).then_inc(s_cin[par], 16)

            def reload(t, par):
                sp.wait_ge(s_ts, t - 1)
                load(t, par)
                sp.wait_ge(s_dif, t - 1)
                load_c(t, par)

            def store(t, par):
                sp.wait_ge(s_out, t + 2)
                sp.dma_start(m.out[bass.ds(t * P, P), :], ob[:, par, :]).then_inc(s_store[par], 16)

            for i in range(2):
                sp.sem_inc(s_store[i], 16)
            for t in range(2):
                load(t, t)
                load_c(t, t)
            reload(2, 0)
            reload(3, 1)
            with sp.Fori(0, NT // 2 - 2) as i:
                for par in range(2):
                    reload(i * 2 + 4 + par, par)
                    store(i * 2 + par, par)
            for t in range(NT - 4, NT):
                store(t, t % 2)
            for i in range(2):
                sp.wait_ge(s_store[i], 16 * NT // 2 + 16)

        @block.gpsimd
        def _(pool):
            pool.memset(ones, 1.0).then_inc(s_const, 1)
            pool.tensor_scalar(fbias, m.rows[:, RBF, :], m.gains[:, 3:4], None, ALU.mult).then_inc(s_const, 1)
            pool.wait_ge(s_const, 2)

            def body(t, par, half, run):
                if run[1]:
                    pool.wait_ge(s_var, t)
                    pool.tensor_tensor(rstd[:, :], var[:, :], m.neghalf[:, 0:1], ALU.pow).then_inc(s_rstd, 1)
                if run[0]:
                    pool.wait_ge(s_scopy, t + 1)
                    if not (isinstance(t, int) and t < 2):
                        pool.wait_ge(s_x3, t - 1)
                    pool.wait_ge(s_cin[par], half * 16 + 16)
                    pool.tensor_tensor(dif[:, par, :], cb[:, par, :], sbuf[:, par, :], ALU.subtract).then_inc(s_dif, 1)
                    pool.tensor_scalar(scaled, sbuf[:, par, :], m.gains[:, 1:2], None, ALU.mult).then_inc(s_scaled, 1)
                    wait_apart(pool, s_scaled, t + 1, m.passed)
                    pool.tensor_tensor(base[:, par, :], xs(t), scaled, ALU.add).then_inc(s_base, 1)
                if run[1]:
                    wait_apart(pool, s_x3, t, m.passed)
                    pool.tensor_tensor(xb[:, 1 - par, :], xs(t - 1), fbias, ALU.add).then_inc(s_xb, 1)

            tiles(pool, body)

        @block.vector
        def _(dve):
            def body(t, par, half, run):
                if run[1]:
                    q = 1 - par
                    dve.wait_ge(s_dif, t)
                    dve.wait_ge(s_sig, t)
                    dve.tensor_tensor(mul, gate, dif[:, q, :], ALU.mult).then_inc(s_mul, 1)
                    dve.wait_ge(s_mul, t)
                    dve.wait_ge(s_base, t)
                    dve.scalar_tensor_tensor(out=xs(t - 1), in0=mul, scalar=m.gains[:, 1:2], in1=base[:, q, :],
                                             op0=ALU.mult, op1=ALU.add).then_inc(s_x3, 1)
                    wait_apart(dve, s_x3, t, m.passed)
                    dve.bn_stats(st[:, :], xs(t - 1)).then_inc(s_st, 1)
                    wait_apart(dve, s_st, t, m.passed)
                    dve.bn_aggr(mv[:, :], st[:, :]).then_inc(s_mv, 1)
                    dve.wait_ge(s_mv, t)
                    dve.tensor_scalar(var[:, :], mv[:, 1:2], EPS, None, ALU.add).then_inc(s_var, 1)
                if run[2]:
                    dve.wait_ge(s_y, t - 1)
                    dve.wait_ge(s_xb, t - 1)
                    dve.wait_ge(s_store[par], half * 16)
                    dve.scalar_tensor_tensor(out=ob[:, par, :], in0=yps[:, 0:D], scalar=m.gains[:, 3:4],
                                             in1=xb[:, par, :], op0=ALU.mult, op1=ALU.add).then_inc(s_out, 1)
                if run[1]:
                    dve.wait_ge(s_rstd, t)
                    if run[2]:
                        dve.wait_ge(s_tx, t - 1)
                    dve.tensor_scalar(xn, xs(t - 1), mv[:, 0:1], rstd[:, :], ALU.subtract, ALU.mult).then_inc(s_norm, 1)

            dve.sem_inc(s_out, 1)
            tiles(dve, body)

        @block.scalar
        def _(act):
            def halves(a):
                return a[:, 0:D].rearrange("p (k n) -> p k n", k=DK)

            def body(t, par, half, run):
                if run[0]:
                    act.wait_ge(s_stretch, t + 1)
                    if not (isinstance(t, int) and t < 2):
                        act.wait_ge(s_base, t - 1)
                    act.copy(sbuf[:, par, :], ips[:, 0:D]).then_inc(s_scopy, 1)
                if run[1]:
                    act.wait_ge(s_gate, t)
                    if run[2]:
                        act.wait_ge(s_mul, t - 1)
                    act.activation(gate, gps[:, 0:D], ACT.Sigmoid).then_inc(s_sig, 1)
                if run[0]:
                    act.wait_ge(s_tc, t + 1)
                    act.copy(gT[:, par, 0:DK, :], halves(cps)).then_inc(s_tccopy, 1)
                if run[2]:
                    act.wait_ge(s_tx, t - 1)
                    act.copy(xT, halves(xps)).then_inc(s_txcopy, 1)
                if run[0]:
                    act.wait_ge(s_ts, t + 1)
                    act.copy(gT[:, par, DK:, :], halves(eps_)).then_inc(s_tscopy, 1)

            warm_up(act, m, ACT.Sigmoid)
            act.sem_inc(s_txcopy, 1)
            tiles(act, body)

        @block.tensor
        def _(pe):
            def body(t, par, half, run):
                first = isinstance(t, int) and t == 0
                if first:
                    pe.wait_ge(s_const, 2)
                if run[0]:
                    pe.wait_ge(s_in[par], half * 32 + 32)
                    if not first:
                        pe.wait_ge(s_scopy, t)
                    pe.matmul(ips[:, 0:D], stretch[:, par, :], win[:, par, :],
                              start=True, stop=True).then_inc(s_stretch, 1)
                if run[1]:
                    pe.wait_ge(s_tscopy, t)
                    if run[2]:
                        pe.wait_ge(s_sig, t - 1)
                    for k in range(2 * DK):
                        pe.matmul(gps[:, 0:D], gT[:, 1 - par, k, :], m.w1[:, 6 * DK + k, :],
                                  start=(k == 0), stop=False)
                    mm = pe.matmul(gps[:, 0:D], ones[0:1, :], m.rows[0:1, RBG, :], start=False, stop=True)
                    mm.then_inc(s_gate, 1)
                if run[0]:
                    pe.wait_ge(s_cin[par], half * 16 + 16)
                    if not first:
                        pe.wait_ge(s_tccopy, t)
                    for k in range(DK):
                        mm = pe.transpose(cps[:, k * P:(k + 1) * P], cb[:, par, k * P:(k + 1) * P], m.ident[:, :])
                    mm.then_inc(s_tc, 1)
                if run[2]:
                    pe.wait_ge(s_norm, t - 1)
                    pe.wait_ge(s_txcopy, t - 1)
                    for k in range(DK):
                        mm = pe.transpose(xps[:, k * P:(k + 1) * P], xn[:, k * P:(k + 1) * P], m.ident[:, :])
                    mm.then_inc(s_tx, 1)
                if run[0]:
                    if not first:
                        pe.wait_ge(s_tscopy, t)
                    for k in range(DK):
                        mm = pe.matmul(eps_[:, k * P:(k + 1) * P], win[:, par, k * P:(k + 1) * P], stretch[:, par, :],
                                       start=True, stop=True)
                    mm.then_inc(s_ts, 1)
                if run[2]:
                    pe.wait_ge(s_txcopy, t)
                    pe.wait_ge(s_out, t - 1)
                    for k in range(DK):
                        mm = pe.matmul(yps[:, 0:D], xT[:, k, :], m.filt[:, k, :], start=(k == 0), stop=(k == DK - 1))
                    mm.then_inc(s_y, 1)

            tiles(pe, body)


STRIDE = 99


def kernel(**inputs):
    import numpy as np
    import concourse.bacc as bacc
    from concourse.bass_utils import run_bass_kernel_spmd

    a = {k: np.asarray(v) for k, v in inputs.items()}

    def tiled(w):
        return w.reshape(-1, P, w.shape[-1]).transpose(1, 0, 2)

    def by_group(w):
        return w.reshape(-1, H // G, G, HD).transpose(0, 1, 3, 2).reshape(w.shape)

    l0 = [by_group(a["L0_xattn_Wq"]), by_group(a["L0_xattn_Wk"]), a["L0_xattn_Wv"], a["L0_xattn_Wo"]]
    l1 = [a["L1_xattn_W" + n].T for n in ("q_c", "k_s", "v_s", "q_s", "k_c", "v_c", "g")]
    cols = [by_group(a["L0_xattn_b" + n]) for n in "qk"]
    cols += [a[n] for n in ("L1_xattn_bk_s", "L1_xattn_bq_s", "L1_xattn_bk_c", "L1_xattn_bq_c")]
    rows = [a[n] for n in ("L0_xattn_bv", "L0_xattn_bo", "L1_xattn_bv_s", "L1_xattn_bv_c", "L1_xattn_bg", "L1_ffn_bias")]
    ctx_T = np.zeros((P, DK, SP_), np.float32)
    ctx_T[:, :, :S] = tiled(a["ctx_1024"][0].T)
    w13 = [a["L0_ffn_" + n].reshape(E, DK, P, F).transpose(0, 2, 1, 3).reshape(E * P, DK * F) for n in ("w1", "w3")]
    w2 = np.zeros((E, NF * P, D), np.float32)
    w2[:, :F] = a["L0_ffn_w2"]
    w2 = w2.reshape(E, NF, P, D).transpose(0, 2, 1, 3).reshape(E * P, NF * D)

    n = np.arange(D)
    angle = 2 * np.pi * ((n[:, None] * n[None, :]) % D) / D
    cos, sin = np.cos(angle), np.sin(angle)
    dft = np.concatenate([tiled(x.astype(np.float32)) for x in (cos, sin, cos / D, sin / D, -sin / D)], axis=1)

    pos = (np.arange(T, dtype=np.float32) + np.float32(0.5)) * np.float32(S / T) - np.float32(0.5)
    pos = np.clip(pos, np.float32(0), np.float32(S - 1))
    lo = np.floor(pos).astype(np.int64)
    hi = np.minimum(lo + 1, S - 1)
    frac = pos - lo.astype(np.float32)
    interp = np.zeros((NT, P, P), np.float32)
    for j in range(T):
        t = j // P
        assert STRIDE * t <= lo[j] and hi[j] < STRIDE * t + P
        interp[t, lo[j] - STRIDE * t, j % P] += np.float32(1) - frac[j]
        interp[t, hi[j] - STRIDE * t, j % P] += frac[j]

    data = {
        "x_in": a["x"][0],
        "ctx_T": ctx_T,
        "w_l0": np.concatenate([tiled(w) for w in l0], axis=1),
        "w_l1": np.concatenate([tiled(w) for w in l1], axis=1),
        "b_cols": np.stack([b.reshape(DK, P).T for b in cols], axis=1),
        "b_rows": np.stack(rows)[None],
        "g_in": np.concatenate([a["g_xattn"], a["g_ffn"]])[None],
        "w_exp": np.concatenate([*w13, w2], axis=1),
        "wf_T": np.concatenate([tiled(a["L1_ffn_w_freq_" + k].T) for k in ("real", "imag")], axis=1),
        "eye": np.eye(P, dtype=np.float32),
        "dft": dft,
        "interp": interp.reshape(NT * P, P),
    }
    nc = bacc.Bacc("TRN2", target_bir_lowering=False, num_devices=1)
    arrays, aps = {}, {}
    for name, x in data.items():
        arrays[name] = np.ascontiguousarray(x)
        aps[name] = nc.dram_tensor(name, x.shape, mybir.dt.from_np(x.dtype), kind="ExternalInput").ap()
    aps["out"] = nc.dram_tensor("out", (T, D), F32, kind="ExternalOutput").ap()
    build(nc, aps)
    r = run_bass_kernel_spmd(nc, [arrays], core_ids=[0])
    return r.results[0]["out"].reshape(1, T, D)
```
